# Optimizing a Trainium2 kernel written in Bass

```python
import numpy as np
import jax
import jax.numpy as jnp

def _softmax(x, axis=-1):
    return jax.nn.softmax(x, axis=axis)

def _gelu(x):
    return jax.nn.gelu(x, approximate=True)

def _silu(x):
    return jax.nn.silu(x)

def _sigmoid(x):
    return jax.nn.sigmoid(x)

def _layernorm(x, axis=-1, eps=1e-05):
    m = jnp.mean(x, axis=axis, keepdims=True)
    v = jnp.var(x, axis=axis, keepdims=True)
    return (x - m) / jnp.sqrt(v + eps)

def _scatter_add(tgt, idx, src, axis=0):
    return tgt.at[idx].add(src)

def _segment_sum(src, seg, n):
    return jax.ops.segment_sum(src, seg, n)
kernel_name = 'mk_adj_preln_d2_adj_r2_ec9bae'

def setup_inputs(seed: int=0):
    np.random.seed(seed)
    _w = jnp.asarray

    def _rec_inputs():
        import jax
        import jax.numpy as jnp
        _gk = jax.random.key(seed)
        x = -0.000125 + 0.9999 * jax.random.normal(jax.random.fold_in(_gk, 1), (32, 256, 512), jnp.float32)
        _w = (1.0 + jnp.arange(256, dtype=jnp.float32)) ** (-0.5)
        _w = _w / _w.mean()
        _pij = jnp.clip(0.0625 * _w[:, None] * _w[None, :], 0.0, 1.0)
        _a = jax.random.uniform(jax.random.fold_in(_gk, 2), (32, 256, 256)) < _pij
        _a = jnp.logical_or(_a, jnp.swapaxes(_a, -1, -2))
        _a = jnp.logical_or(_a, jnp.eye(256, dtype=bool))
        _af = _a.astype(jnp.float32)
        _af = _af * jax.random.uniform(jax.random.fold_in(_gk, 3), (32, 256, 256), jnp.float32, 0.05, 0.999994)
        adj = _af
        return (x, adj)
    x, adj = _rec_inputs()

    def _L0_gnn_setup():
        import jax, jax.numpy as jnp
        import numpy as np
        B, N, H, E = (64, 256, 512, 4)
        BN_EPS = 1e-05
        key = jax.random.key(seed)
        ks = jax.random.split(key, 6)
        x = jax.random.normal(ks[0], (B, N, H), dtype=jnp.float32)
        adj = jax.random.uniform(ks[1], (B, N, N), dtype=jnp.float32)
        stdv = 1.0 / np.sqrt(H)
        expert_w = jax.random.uniform(ks[2], (E, H, H), minval=-stdv, maxval=stdv, dtype=jnp.float32)
        r_std = 1.0 / np.sqrt(H)
        router_w = jax.random.uniform(ks[3], (H, E), minval=-r_std, maxval=r_std, dtype=jnp.float32)
        router_b = jax.random.uniform(ks[4], (E,), minval=-r_std, maxval=r_std, dtype=jnp.float32)
        bn_gamma = jnp.ones((E, H), dtype=jnp.float32)
        bn_beta = jnp.zeros((E, H), dtype=jnp.float32)
        return {'x': x, 'adj': adj, 'router_w': router_w, 'router_b': router_b, 'expert_w': expert_w, 'bn_gamma': bn_gamma, 'bn_beta': bn_beta}
    _L0_gnn_all = _L0_gnn_setup()
    _L0_gnn_in = {k: v for k, v in _L0_gnn_all.items() if k in ('router_w', 'router_b', 'expert_w', 'bn_gamma', 'bn_beta')}
    del _L0_gnn_all

    def _L1_gnn_setup():
        import jax, jax.numpy as jnp
        import numpy as np
        NUM_HEADS = 16
        key = jax.random.key(seed)
        ks = jax.random.split(key, 7)
        B, N, D = (16, 256, 512)
        return {'x': jax.random.normal(ks[0], (B, N, D), dtype=jnp.float32), 'spatial_encoding': jax.random.normal(ks[1], (B, N, N), dtype=jnp.float32), 'edge_encoding': jax.random.normal(ks[2], (B, N, N), dtype=jnp.float32), 'Wq': jax.random.normal(ks[3], (D, D), dtype=jnp.float32) * D ** (-0.5), 'Wk': jax.random.normal(ks[4], (D, D), dtype=jnp.float32) * D ** (-0.5), 'Wv': jax.random.normal(ks[5], (D, D), dtype=jnp.float32) * D ** (-0.5), 'Wo': jax.random.normal(ks[6], (D, D), dtype=jnp.float32) * D ** (-0.5)}
    _L1_gnn_all = _L1_gnn_setup()
    _L1_gnn_in = {k: v for k, v in _L1_gnn_all.items() if k in ('Wq', 'Wk', 'Wv', 'Wo')}
    del _L1_gnn_all
    return {'x': x, 'adj': adj, 'L0_gnn_router_w': _L0_gnn_in['router_w'], 'L0_gnn_router_b': _L0_gnn_in['router_b'], 'L0_gnn_expert_w': _L0_gnn_in['expert_w'], 'L0_gnn_bn_gamma': _L0_gnn_in['bn_gamma'], 'L0_gnn_bn_beta': _L0_gnn_in['bn_beta'], 'L1_gnn_Wq': _L1_gnn_in['Wq'], 'L1_gnn_Wk': _L1_gnn_in['Wk'], 'L1_gnn_Wv': _L1_gnn_in['Wv'], 'L1_gnn_Wo': _L1_gnn_in['Wo']}

def reference(x, adj, L0_gnn_router_w, L0_gnn_router_b, L0_gnn_expert_w, L0_gnn_bn_gamma, L0_gnn_bn_beta, L1_gnn_Wq, L1_gnn_Wk, L1_gnn_Wv, L1_gnn_Wo):
    import jax
    import jax.numpy as jnp

    def _L0_gnn_ref(x, adj, router_w, router_b, expert_w, bn_gamma, bn_beta):
        import jax, jax.numpy as jnp
        import numpy as np
        B, N, H, E = (64, 256, 512, 4)
        BN_EPS = 1e-05
        scores = x.mean(axis=1) @ router_w + router_b
        top1 = jnp.argmax(scores, axis=-1)
        n_exp = expert_w.shape[0]
        W = expert_w[top1]
        support = jnp.einsum('bnh,bhk->bnk', x, W)
        out = jnp.einsum('bnm,bmk->bnk', adj, support)
        s = jax.ops.segment_sum(out.sum(axis=1), top1, num_segments=n_exp)
        ss = jax.ops.segment_sum((out * out).sum(axis=1), top1, num_segments=n_exp)
        cnt = jax.ops.segment_sum(jnp.ones_like(top1, dtype=out.dtype), top1, num_segments=n_exp) * out.shape[1]
        cnt = jnp.maximum(cnt, 1.0)[:, None]
        mean = s / cnt
        var = ss / cnt - mean * mean
        m = mean[top1][:, None, :]
        inv = jax.lax.rsqrt(var[top1][:, None, :] + BN_EPS)
        y = (out - m) * inv * bn_gamma[top1][:, None, :] + bn_beta[top1][:, None, :]
        return jax.nn.relu(y)

    def _L1_gnn_ref(x, spatial_encoding, edge_encoding, Wq, Wk, Wv, Wo):
        import jax, jax.numpy as jnp
        import numpy as np
        NUM_HEADS = 16
        B, N, D = x.shape
        H = NUM_HEADS
        hd = D // H
        scale = D ** (-0.5)

        def split_heads(t):
            return t.reshape(B, N, H, hd).transpose(0, 2, 1, 3)
        q = split_heads(x @ Wq.T)
        k = split_heads(x @ Wk.T)
        v = split_heads(x @ Wv.T)
        bias = (spatial_encoding + edge_encoding)[:, None]
        a = jnp.einsum('bhnd,bhmd->bhnm', q, k) * scale + bias
        row_nonzero = jnp.any(a != 0, axis=-1, keepdims=True)
        a = jnp.where(row_nonzero, a, -jnp.inf)
        p = jax.nn.softmax(a, axis=-1)
        p = jnp.where(jnp.isnan(p), 0.0, p)
        o = jnp.einsum('bhnm,bhmd->bhnd', p, v)
        o = o.transpose(0, 2, 1, 3).reshape(B, N, D)
        return o @ Wo.T
    h = jnp.maximum(_layernorm(x, axis=-1), 0.0)
    x = x + _L0_gnn_ref(h, adj, L0_gnn_router_w, L0_gnn_router_b, L0_gnn_expert_w, L0_gnn_bn_gamma, L0_gnn_bn_beta)
    h = jnp.maximum(_layernorm(x, axis=-1), 0.0)
    x = x + _L1_gnn_ref(h, adj, adj, L1_gnn_Wq, L1_gnn_Wk, L1_gnn_Wv, L1_gnn_Wo)
    return x

_drawn_inputs = setup_inputs


def setup_inputs(seed=0):
    import zlib

    import numpy as np

    out = dict(_drawn_inputs(seed))
    spreads = {'L0_gnn_bn_gamma': (1.0, 0.2), 'L0_gnn_bn_beta': (0.0, 0.1)}
    factors = {'L1_gnn_Wq': 8.0, 'L1_gnn_Wk': 8.0}
    for name, (base, spread) in spreads.items():
        noise = np.random.default_rng([zlib.crc32(name.encode()), seed]).standard_normal(out[name].shape)
        drawn = base * np.exp(spread * noise) if base else spread * noise
        out[name] = jnp.asarray(drawn.astype(out[name].dtype))
    for name, factor in factors.items():
        out[name] = (out[name] * factor).astype(out[name].dtype)
    return out
```

```python
from contextlib import ExitStack

import concourse.bass as bass
from concourse import mybir

F32 = mybir.dt.float32
F32R = mybir.dt.float32r
BF16 = mybir.dt.bfloat16
F16 = mybir.dt.float16
U32 = mybir.dt.uint32
ALU = mybir.AluOpType
ACT = mybir.ActivationFunctionType
AX_X = mybir.AxisListType.X

P = 128
B = 32
N = 256
D = 512
E = 4
H = 16
HD = D // H
NT = N // P
KT = D // P
HPT = P // HD
PAIRS = B // 2
SCALE = float(D) ** -0.5
LN_EPS = 1e-5
BN_EPS = 1e-5
BIG = 3.0e38
HALF = KT // 2
VW = 3 * HD + 2
LEAD = 4
FIRST = 4

HILO = ((0, 0), (0, 1), (1, 0))


def build(nc, x, adj, adj_t, router_w, router_b, expert_w, gamma, beta, attn_w, out):
    with ExitStack() as ctx:
        def sem(name):
            return ctx.enter_context(nc.semaphore(name))

        scratch = nc.dram_tensor("out_t_scratch", (B, P, KT * N), F32, kind="Internal").ap()
        x_rows = x.rearrange("b (t p) d -> b p t d", p=P)
        out_rows = out.rearrange("b (t p) d -> b p t d", p=P)
        adj_rows = adj.rearrange("b (t p) m -> b p t m", p=P)
        adj_t_rows = adj_t.rearrange("b (t p) n -> b p t n", p=P)
        expert_rows = expert_w.rearrange("e (f k p) d -> (e f) p k d", f=2, p=P)
        attn_rows = attn_w.rearrange("w (k p) d -> (w k) p d", p=P)

        def sb(name, shape, dt=F32, stack=ctx):
            return stack.enter_context(nc.sbuf_tensor(name, shape, dt))

        attn_hi = sb("attn_hi", [P, 4 * KT, D], F32R)
        attn_lo = sb("attn_lo", [P, 4 * KT, D], F32R)
        ident = sb("ident", [P, P])
        ident16 = sb("ident16", [P, P], F16)
        neg_half = sb("neg_half", [P, 2])
        out_moments = sb("out_moments", [P, B, KT, 6])
        top1_row = sb("top1_row", [1, B])
        bn_apply = sb("bn_apply", [P, 2, B, KT])

        def ps(name, shape, dt=F32, stack=ctx):
            return stack.enter_context(nc.psum_tensor(name, shape, dt))

        ident_zero = sem("ident_zero")
        ident_ready = sem("ident_ready")
        small_landed = sem("small_landed")
        raw_w_landed = [sem(f"raw_w_landed{s}") for s in range(2)]
        expert_hi_ready = sem("expert_hi_ready")
        expert_lo_ready = sem("expert_lo_ready")
        pads_ready = sem("pads_ready")
        x_landed = [sem(f"x_landed{u}") for u in range(2)]
        adj_t_landed = [sem(f"adj_t_landed{u}") for u in range(2)]
        attn_raw_landed = sem("attn_raw_landed")
        attn_hi_ready = sem("attn_hi_ready")
        attn_lo_ready = sem("attn_lo_ready")
        partials_ready = sem("partials_ready")
        moments_ready = sem("moments_ready")
        pool_step = sem("pool_step")
        ln_ready = sem("ln_ready")
        h_ready = sem("h_ready")
        ht_in_psum = sem("ht_in_psum")
        ht_hi_ready = sem("ht_hi_ready")
        ht_lo_ready = sem("ht_lo_ready")
        logits_in_psum = sem("logits_in_psum")
        logits_ready = sem("logits_ready")
        best_ready = sem("best_ready")
        index_ready = sem("index_ready")
        support_in_psum = sem("support_in_psum")
        support_hi_ready = sem("support_hi_ready")
        support_lo_ready = sem("support_lo_ready")
        adj_hi_ready = sem("adj_hi_ready")
        adj_ready = sem("adj_ready")
        out_in_psum = sem("out_in_psum")
        out_t_ready = sem("out_t_ready")
        out_moments_ready = sem("out_moments_ready")
        out_t_stored = [sem(f"out_t_stored{u}") for u in range(2)]
        top1_spread = sem("top1_spread")
        bn_step = sem("bn_step")
        bn_var_ready = sem("bn_var_ready")
        bn_inv_step = sem("bn_inv_step")
        bn_ready = sem("bn_ready")

        def wait_past(eng, which, value):
            if not isinstance(value, int) or value > 0:
                eng.wait_ge(which, value)

        waits_passed = sem("waits_passed")

        def wait_alone(eng, which, value):
            eng.wait_ge(which, value)
            eng.sem_inc(waits_passed, 1)

        with ExitStack() as one:
            expert_hi = sb("expert_hi", [P, E * KT, D], F32R, one)
            expert_lo = sb("expert_lo", [P, E * KT, D], F32R, one)
            raw_w = sb("raw_w", [P, 2, HALF, D], F32, one)
            attn_raw = raw_w[:, 0, 0, :]
            router = sb("router", [P, KT, E], F32, one)
            router_bias = sb("router_bias", [1, E], F32, one)
            bn_gb = sb("bn_gb", [P, 2, E, KT], F32, one)
            x_in = sb("x_in", [P, 2, NT, D], F32, one)
            adj_t_in = sb("adj_t_in", [P, 2, NT, N], F32, one)
            adj_t_hl = sb("adj_t_hl", [P, 2, 2, NT, N], F32R, one)
            partials = sb("partials", [P, NT, 6], F32, one)
            moments = sb("moments", [P, 2, NT, 2], F32, one)
            ln_tmp = sb("ln_tmp", [P, 2, NT], F32, one)
            ln_scale = sb("ln_scale", [P, 2, NT], F32, one)
            ln_shift = sb("ln_shift", [P, 2, NT], F32, one)
            h = sb("h", [P, 2, NT, D], F32, one)
            ht_hl = sb("ht_hl", [P, 2, 2, KT, N], F32R, one)
            h_sum = sb("h_sum", [P, 2, KT], F32, one)
            logits = sb("logits", [1, 8], F32, one)
            best = sb("best", [1, 8], F32, one)
            index = sb("index", [1, 2, 8], U32, one)
            support_hl = sb("support_hl", [P, 2, NT, D], F32R, one)
            out_t = sb("out_t", [P, 2, KT, N], F32, one)
            ones_row = sb("ones_row", [1, P], F32, one)
            x_flat = x_in[:].rearrange("p u t d -> p (u t d)")
            taken = [0]

            def tmp(*shape):
                size = 1
                for s in shape:
                    size *= s
                taken[0] += size
                names = " ".join("abcd"[:len(shape)])
                return x_flat[:, taken[0] - size:taken[0]].rearrange(f"p ({names}) -> p {names}", **dict(zip("abcd", shape)))

            top1_all = tmp(B)
            onehot = tmp(E, B)
            gsum = tmp(2, KT, B)
            pick = tmp(E, KT, B)
            gtmp = tmp(2, KT, B)
            esum = tmp(2, E, KT)
            ecount = tmp(E)
            emean = tmp(2, E, KT)
            evar = tmp(E, KT)
            einv = tmp(E, KT)
            eab = tmp(2, E, KT)
            etmp = tmp(E, KT)
            bn_half = sb("bn_half", [P, E, KT], F32, one)
            ps_ht = ps("ps_ht", [P, KT, N], F32, one)
            ps_support = ps("ps_support", [P, NT, D], F32, one)
            ps_out = ps("ps_out", [P, KT, N], F32, one)
            ps_small = ps("ps_small", [P, 512], F32, one)

            block = one.enter_context(nc.Block())

            @block.sync
            def _(sp):
                def load_x(i, u):
                    sp.dma_start(x_in[:, u], x_rows[2 * i + u]).then_inc(x_landed[u], 16)

                def load_adj(i, u):
                    sp.dma_start(adj_t_in[:, u], adj_t_rows[2 * i + u]).then_inc(adj_t_landed[u], 16)

                load_x(0, 0)
                for f in range(2):
                    sp.dma_start(raw_w[:, f], expert_rows[f]).then_inc(raw_w_landed[f], 16)
                sp.dma_start(router[:], router_w.rearrange("(k p) e -> p k e", p=P)).then_inc(small_landed, 16)
                sp.dma_start(router_bias[:], router_b).then_inc(small_landed, 16)
                sp.dma_start(bn_gb[:, 0], gamma).then_inc(small_landed, 16)
                sp.dma_start(bn_gb[:, 1], beta).then_inc(small_landed, 16)
                load_x(0, 1)
                load_adj(0, 0)
                load_adj(0, 1)
                sp.wait_ge(h_ready, 1)
                load_x(1, 0)
                for f in range(2, 2 * E):
                    sp.wait_ge(expert_lo_ready, HALF * (f - 1))
                    sp.dma_start(raw_w[:, f % 2], expert_rows[f]).then_inc(raw_w_landed[f % 2], 16)
                sp.wait_ge(expert_lo_ready, KT * E)

                def pair(i, last):
                    wait_past(sp, attn_lo_ready, i)
                    sp.dma_start(attn_raw, attn_rows[i]).then_inc(attn_raw_landed, 16)
                    for u in range(2):
                        b = 2 * i + u
                        if not last:
                            sp.wait_ge(adj_ready, b + 1)
                            load_adj(i + 1, u)
                        if not last and u == 0:
                            sp.wait_ge(h_ready, b + 2)
                            load_x(i + 1, 1)
                        if u == 1 and (not isinstance(i, int) or i < PAIRS - 2):
                            sp.wait_ge(h_ready, b + 2)
                            load_x(i + 2, 0)
                        sp.wait_ge(out_t_ready, b + 1)
                        sp.dma_start(scratch[b], out_t[:, u].rearrange("p k n -> p (k n)")).then_inc(out_t_stored[u], 16)

                pair(0, False)
                with sp.Fori(1, PAIRS - 2) as i:
                    pair(i, False)
                pair(PAIRS - 2, False)
                pair(PAIRS - 1, True)
                for u in range(2):
                    sp.wait_ge(out_t_stored[u], 16 * PAIRS)

            @block.gpsimd
            def _(pool):
                pool.memset(ident[:], 0.0)
                pool.memset(ident16[:], 0.0)
                pool.memset(neg_half[:], -0.5)
                pool.memset(bn_half[:], -0.5).then_inc(ident_zero, 1)
                pool.wait_ge(ident_zero, 1)
                for m in (ident, ident16):
                    last_op = pool.affine_select(out=m[:], in_=m[:], compare_op=ALU.not_equal, fill=1.0, base=0,
                                                 pattern=[[-1, P]], channel_multiplier=1)
                last_op.then_inc(ident_ready, 1)

                def normaliser(i, u):
                    b = 2 * i + u
                    wait_past(pool, ln_ready, b)
                    wait_alone(pool, moments_ready, b + 1)
                    pool.tensor_scalar(ln_tmp[:, 0], moments[:, u, :, 1], LN_EPS, 1.0, ALU.add, ALU.mult)
                    pool.tensor_scalar(ln_tmp[:, 1], moments[:, u, :, 0], -1.0, 1.0, ALU.mult, ALU.mult).then_inc(pool_step, 1)
                    pool.wait_ge(pool_step, 2 * b + 1)
                    pool.tensor_tensor(ln_scale[:, u], ln_tmp[:, 0], neg_half[:], ALU.pow).then_inc(pool_step, 1)
                    pool.wait_ge(pool_step, 2 * b + 2)
                    pool.tensor_tensor(ln_shift[:, u], ln_tmp[:, 1], ln_scale[:, u], ALU.mult).then_inc(ln_ready, 1)

                def split_adj(i, u):
                    b = 2 * i + u
                    wait_alone(pool, adj_t_landed[u], 16 * (i + 1))
                    pool.tensor_copy(adj_t_hl[:, u, 0], adj_t_in[:, u]).then_inc(adj_hi_ready, 1)
                    pool.wait_ge(adj_hi_ready, b + 1)
                    pool.tensor_tensor(adj_t_hl[:, u, 1], adj_t_in[:, u], adj_t_hl[:, u, 0].bitcast(F32),
                                       ALU.subtract).then_inc(adj_ready, 1)

                def split_attn(i):
                    wait_alone(pool, attn_raw_landed, 16 * (i + 1))
                    pool.tensor_copy(attn_hi[:, i], attn_raw).then_inc(attn_hi_ready, 1)
                    pool.wait_ge(attn_hi_ready, i + 1)
                    pool.tensor_tensor(attn_lo[:, i], attn_raw, attn_hi[:, i].bitcast(F32),
                                       ALU.subtract).then_inc(attn_lo_ready, 1)

                normaliser(0, 0)
                normaliser(0, 1)
                split_adj(0, 0)
                split_adj(0, 1)

                def pair(i, last):
                    for u in range(2):
                        b = 2 * i + u
                        if not last:
                            normaliser(i + 1, u)
                        if u == 0:
                            split_attn(i)
                        if not last:
                            wait_alone(pool, out_in_psum, b + 1)
                            split_adj(i + 1, u)

                pair(0, False)
                with pool.Fori(1, PAIRS - 1) as i:
                    pair(i, False)
                pair(PAIRS - 1, True)

                pool.wait_ge(bn_var_ready, 1)
                pool.tensor_tensor(einv, evar, bn_half[:], ALU.pow).then_inc(bn_inv_step, 1)

            @block.scalar
            def _(act):
                def split_expert(f):
                    act.wait_ge(raw_w_landed[f % 2], 16 * (f // 2 + 1))
                    for k in range(HALF):
                        act.activation(expert_hi[:, HALF * f + k], raw_w[:, f % 2, k], ACT.Copy).then_inc(expert_hi_ready, 1)

                def normalise(i, u):
                    act.wait_ge(ln_ready, 2 * i + u + 1)
                    for t in range(NT):
                        op = act.activation(h[:, u, t], x_in[:, u, t], ACT.Relu, bias=ln_shift[:, u, t:t + 1],
                                            scale=ln_scale[:, u, t:t + 1])
                    op.then_inc(h_ready, 1)

                def ht_high(i, u):
                    act.wait_ge(ht_in_psum, 2 * i + u + 1)
                    for k in range(KT):
                        act.activation(ht_hl[:, u, 0, k], ps_ht[:, k], ACT.Copy,
                                       accum_out=h_sum[:, u, k:k + 1]).then_inc(ht_hi_ready, 1)

                normalise(0, 0)
                split_expert(0)
                ht_high(0, 0)
                normalise(0, 1)
                for f in range(1, 2 * E):
                    split_expert(f)

                def pair(i, last):
                    for u in range(2):
                        b = 2 * i + u
                        ni, nu = (i, 1) if u == 0 else (i + 1, 0)
                        more = u == 0 or not last
                        wait_past(act, out_in_psum, b)
                        for t in range(NT):
                            act.wait_ge(support_in_psum, NT * b + t + 1)
                            act.activation(support_hl[:, 0, t], ps_support[:, t], ACT.Copy).then_inc(support_hi_ready, 1)
                        if more:
                            ht_high(ni, nu)
                        if not last:
                            normalise(i + 1, u)
                        act.wait_ge(out_in_psum, b + 1)
                        wait_past(act, out_t_stored[u], 16 * i)
                        act.activation(out_t[:, u], ps_out[:], ACT.Copy).then_inc(out_t_ready, 1)

                pair(0, False)
                with act.Fori(1, PAIRS - 1) as i:
                    pair(i, False)
                pair(PAIRS - 1, True)

            @block.vector
            def _(dve):
                def row_moments(i, u):
                    wait_past(dve, moments_ready, 2 * i + u)
                    dve.wait_ge(x_landed[u], 16 * (i + 1))
                    for t in range(NT):
                        op = dve.bn_stats(partials[:, t], x_in[:, u, t])
                    op.then_inc(partials_ready, 1)
                    wait_alone(dve, partials_ready, 2 * i + u + 1)
                    for t in range(NT):
                        op = dve.bn_aggr(moments[:, u, t], partials[:, t])
                    op.then_inc(moments_ready, 1)

                def ht_low(i, u):
                    for k in range(0, KT, HALF):
                        dve.wait_ge(ht_hi_ready, KT * (2 * i + u) + k + HALF)
                        dve.tensor_tensor(ht_hl[:, u, 1, k:k + HALF], ps_ht[:, k:k + HALF],
                                          ht_hl[:, u, 0, k:k + HALF].bitcast(F32), ALU.subtract).then_inc(ht_lo_ready, 1)

                def choose(i, u):
                    b = 2 * i + u
                    wait_past(dve, index_ready, b)
                    dve.wait_ge(logits_in_psum, b + 1)
                    dve.scalar_tensor_tensor(out=logits[0:1, 0:E], in0=ps_small[0:1, 0:E], scalar=1.0 / N,
                                             in1=router_bias[:], op0=ALU.mult, op1=ALU.add).then_inc(logits_ready, 1)
                    wait_alone(dve, logits_ready, b + 1)
                    dve.max(best[:], logits[:]).then_inc(best_ready, 1)
                    wait_alone(dve, best_ready, b + 1)
                    dve.max_index(index[:, u], best[:], logits[:]).then_inc(index_ready, 1)
                    dve.wait_ge(index_ready, b + 1)
                    dve.tensor_copy(top1_row[0:1, bass.ds(b, 1)], index[:, u, 0:1])

                dve.memset(logits[:], -BIG)
                dve.memset(ones_row[:], 1.0).then_inc(pads_ready, 1)
                dve.wait_ge(pads_ready, 1)
                dve.wait_ge(small_landed, 64)
                row_moments(0, 0)
                row_moments(0, 1)
                ht_low(0, 0)
                for f in range(2 * E):
                    for k in range(HALF):
                        dve.wait_ge(expert_hi_ready, HALF * f + k + 1)
                        dve.tensor_tensor(expert_lo[:, HALF * f + k], raw_w[:, f % 2, k],
                                          expert_hi[:, HALF * f + k].bitcast(F32), ALU.subtract).then_inc(expert_lo_ready, 1)
                choose(0, 0)

                def pair(i, last):
                    for u in range(2):
                        b = 2 * i + u
                        ni, nu = (i, 1) if u == 0 else (i + 1, 0)
                        more = u == 0 or not last
                        for t in range(NT):
                            dve.wait_ge(support_hi_ready, NT * b + t + 1)
                            dve.tensor_tensor(support_hl[:, 1, t], ps_support[:, t], support_hl[:, 0, t].bitcast(F32),
                                              ALU.subtract).then_inc(support_lo_ready, 1)
                            if t == 0 and not last:
                                row_moments(i + 1, u)
                        if more:
                            ht_low(ni, nu)
                            choose(ni, nu)
                        dve.wait_ge(out_t_ready, b + 1)
                        for k in range(KT):
                            op = dve.bn_stats(out_moments[:, b, k], out_t[:, u, k])
                        op.then_inc(out_moments_ready, 1)

                pair(0, False)
                with dve.Fori(1, PAIRS - 1) as i:
                    pair(i, False)
                pair(PAIRS - 1, True)

                step = [0]

                def then(op):
                    step[0] += 1
                    op.then_inc(bn_step, 1)
                    dve.wait_ge(bn_step, step[0])

                dve.wait_ge(out_moments_ready, B)
                dve.wait_ge(top1_spread, 1)
                then(dve.tensor_copy(top1_all, ps_small[:, 0:B]))
                for e in range(E):
                    op = dve.tensor_scalar(onehot[:, e], top1_all, float(e), None, ALU.is_equal)
                then(op)
                m = out_moments[:].rearrange("p b k s -> p s k b")
                half = float(N // 2)
                dve.tensor_tensor(gtmp[:, 0], m[:, 1], m[:, 1], ALU.mult)
                dve.tensor_tensor(gtmp[:, 1], m[:, 4], m[:, 4], ALU.mult)
                then(dve.tensor_tensor(gsum[:, 0], m[:, 1], m[:, 4], ALU.add))
                then(dve.tensor_tensor(gtmp[:, 0], gtmp[:, 0], gtmp[:, 1], ALU.add))
                then(dve.tensor_tensor(gsum[:, 1], m[:, 2], m[:, 5], ALU.add))
                dve.tensor_scalar(gsum[:, 0], gsum[:, 0], half, None, ALU.mult)
                then(dve.scalar_tensor_tensor(out=gsum[:, 1], in0=gtmp[:, 0], scalar=half, in1=gsum[:, 1],
                                              op0=ALU.mult, op1=ALU.add))
                mask = onehot.unsqueeze(2).to_broadcast([P, E, KT, B])
                for s in range(2):
                    then(dve.tensor_tensor(pick, gsum[:, s].unsqueeze(1).to_broadcast([P, E, KT, B]), mask, ALU.mult))
                    then(dve.tensor_reduce(esum[:, s], pick, AX_X, ALU.add))
                then(dve.tensor_reduce(ecount, onehot, AX_X, ALU.add))
                then(dve.tensor_scalar(ecount, ecount, float(N), 1.0, ALU.mult, ALU.max))
                then(dve.reciprocal(ecount, ecount))
                for s in range(2):
                    then(dve.tensor_tensor(emean[:, s], esum[:, s], ecount.unsqueeze(2).to_broadcast([P, E, KT]), ALU.mult))
                then(dve.tensor_tensor(etmp, emean[:, 0], emean[:, 0], ALU.mult))
                then(dve.tensor_tensor(evar, emean[:, 1], etmp, ALU.subtract))
                dve.tensor_scalar(evar, evar, BN_EPS, None, ALU.add).then_inc(bn_var_ready, 1)
                dve.wait_ge(bn_inv_step, 1)
                then(dve.tensor_tensor(eab[:, 0], einv, bn_gb[:, 0], ALU.mult))
                then(dve.tensor_tensor(etmp, emean[:, 0], eab[:, 0], ALU.mult))
                then(dve.tensor_tensor(eab[:, 1], bn_gb[:, 1], etmp, ALU.subtract))
                for s in range(2):
                    pv = pick.rearrange("p e k b -> p (e k b)").rearrange("p (b k e) -> p b k e", b=B, k=KT)
                    then(dve.tensor_tensor(pv, onehot.rearrange("p e b -> p b e").unsqueeze(2).to_broadcast([P, B, KT, E]),
                                           eab[:, s].rearrange("p e k -> p k e").unsqueeze(1).to_broadcast([P, B, KT, E]), ALU.mult))
                    then(dve.tensor_reduce(bn_apply[:, s], pv, AX_X, ALU.add))

            @block.tensor
            def _(pe):
                chosen = pe.alloc_register("chosen_expert")

                def transpose_h(i, u):
                    b = 2 * i + u
                    pe.wait_ge(h_ready, b + 1)
                    wait_past(pe, ht_lo_ready, KT // HALF * b)
                    for k in range(KT):
                        for t in range(NT):
                            op = pe.transpose(ps_ht[:, k, t * P:(t + 1) * P], h[:, u, t, k * P:(k + 1) * P], ident[:])
                    op.then_inc(ht_in_psum, 1)

                def route(i, u):
                    b = 2 * i + u
                    pe.wait_ge(ht_hi_ready, KT * (b + 1))
                    wait_past(pe, index_ready, b)
                    for k in range(KT):
                        op = pe.matmul(ps_small[0:1, 0:E], h_sum[:, u, k:k + 1], router[:, k], start=(k == 0), stop=(k == KT - 1))
                    op.then_inc(logits_in_psum, 1)

                def support(i, u, t, w):
                    b = 2 * i + u
                    wait_past(pe, support_lo_ready, NT * b)
                    for n, (s, m) in enumerate(HILO):
                        if (s, m) == (1, 0):
                            pe.wait_ge(ht_lo_ready, KT // HALF * (b + 1))
                        for k in range(KT):
                            weights = (expert_hi, expert_lo)[m]
                            op = pe.matmul(ps_support[:, t], ht_hl[:, u, s, k, t * P:(t + 1) * P],
                                           weights[:, bass.ds(w + k, 1), :].rearrange("p o d -> p (o d)"),
                                           start=(n == 0 and k == 0), stop=(n == 2 and k == KT - 1))
                    op.then_inc(support_in_psum, 1)

                def aggregate(i, u, tiles):
                    b = 2 * i + u
                    pe.wait_ge(adj_ready, b + 1)
                    wait_past(pe, out_t_ready, b)
                    pe.wait_ge(support_lo_ready, NT * (b + 1))
                    for k in tiles:
                        for n, (s, m) in enumerate(HILO):
                            for t in range(NT):
                                op = pe.matmul(ps_out[:, k], support_hl[:, s, t, k * P:(k + 1) * P], adj_t_hl[:, u, m, t],
                                               start=(n == 0 and t == 0), stop=(n == 2 and t == NT - 1))
                    if k == KT - 1:
                        op.then_inc(out_in_psum, 1)

                pe.wait_ge(ident_ready, 1)
                transpose_h(0, 0)
                pe.wait_ge(small_landed, 64)
                route(0, 0)
                pe.wait_ge(expert_lo_ready, KT * E)

                def pair(i, last):
                    for u in range(2):
                        b = 2 * i + u
                        ni, nu = (i, 1) if u == 0 else (i + 1, 0)
                        more = u == 0 or not last
                        wait_alone(pe, index_ready, b + 1)
                        pe.reg_load(chosen, index[0:1, u, 0:1])
                        w = pe.snap(chosen, min_val=0, max_val=E - 1) * KT
                        support(i, u, 0, w)
                        support(i, u, 1, w)
                        if more:
                            transpose_h(ni, nu)
                        aggregate(i, u, range(HALF))
                        if more:
                            route(ni, nu)
                        aggregate(i, u, range(HALF, KT))

                pair(0, False)
                with pe.Fori(1, PAIRS - 1) as i:
                    pair(i, False)
                pair(PAIRS - 1, True)
                pe.wait_ge(out_moments_ready, B)
                pe.matmul(ps_small[:, 0:B], ones_row[:], top1_row[:], start=True, stop=True).then_inc(top1_spread, 1)

        phase_two(nc, ctx, wait_alone, wait_past, x_rows, adj_rows, scratch, out_rows, attn_hi, attn_lo, ident, ident16, neg_half, bn_apply)


AT_Y = 4
AT_QK3 = (5, 6)
AT_NORM = 6
AT_H = 7
AT_QK = {0: (8, 9), 1: (13, 14), 2: (15, 16)}
AT_V = {0: (10, 10), 1: (11, 12)}
AT_O = 17
AT_PROJECT = {18: 0, 19: 1}
AT_BIAS = 17
AT_APPLY = 18


def phase_two(nc, ctx, wait_alone, wait_past, x_rows, adj_rows, scratch, out_rows, attn_hi, attn_lo, ident, ident16,
              neg_half, bn_apply):
    def sem(name):
        return ctx.enter_context(nc.semaphore(name))

    def sb(name, shape, dt=F32):
        return ctx.enter_context(nc.sbuf_tensor(name, shape, dt))

    def ps(name, shape, dt=F32):
        return ctx.enter_context(nc.psum_tensor(name, shape, dt))

    x_in = sb("x2_in", [P, 2, NT, D])
    y = sb("y", [P, 2, KT, N])
    adj_in = sb("adj_in", [P, NT, N])
    bias = sb("bias", [P, 2, NT, N])
    scale_shift = sb("scale_shift", [P, 2, KT])
    x1 = sb("x1", [P, 2, NT, D])
    partials = sb("partials2", [P, NT, 6])
    moments = sb("moments2", [P, NT, 2])
    ln_tmp = sb("ln_tmp2", [P, 2, NT])
    ln_scale = sb("ln_scale2", [P, NT])
    ln_shift = sb("ln_shift2", [P, NT])
    h2 = sb("h2", [P, NT, D])
    h2t = sb("h2t", [P, 2, KT, N], F32R)
    q = sb("q", [P, 2, 2, KT, N], F32R)
    k_ = sb("k", [P, 2, 2, KT, N], F32R)
    v = sb("v", [P, 2, NT, H, VW], BF16)
    v_rest = sb("v_rest", [P, NT, D])
    a = sb("a", [P, 2, NT, N])
    least = sb("least", [P, 4, NT])
    nonzero = sb("nonzero", [P, 2, NT, H])
    prob = sb("prob", [P, 4, NT, N])
    prob16 = sb("prob16", [P, 4, 2, NT, N], F16)
    pt = sb("pt", [P, 2, 2, NT, N], F16)
    o_raw = sb("o_raw", [P, NT, 4, HD])
    row_sum = sb("row_sum", [P, NT, 4])
    row_scale = sb("row_scale", [P, NT, 4])
    o = sb("o", [P, NT, H, HD])
    ot = sb("ot", [P, 2, KT, N], F32R)
    result = sb("result", [P, 2, NT, D])

    ps_g = ps("ps_g", [P, 2, 512])
    ps_s = ps("ps_s", [P, 2, NT, N])
    ps_pt = ps("ps_pt", [P, 2, 2, NT, N], F16)
    ps_o = ps("ps_o", [P, NT, 512])

    landed = [sem(f"graph_landed{u}") for u in range(2)]
    adj_landed = sem("adj_landed")
    ones_ready = sem("ones_ready")
    bias_ready = sem("bias_ready")
    scale_shift_ready = sem("scale_shift_ready")
    y_ready = sem("y_ready")
    y_in_psum = sem("y_in_psum")
    x1_ready = sem("x1_ready")
    partials_ready = sem("partials2_ready")
    moments_ready = sem("moments2_ready")
    pool_step = sem("pool2_step")
    ln_ready = sem("ln2_ready")
    h2_ready = sem("h2_ready")
    h2t_in_psum = sem("h2t_in_psum")
    h2t_hi_ready = sem("h2t_hi_ready")
    h2t_lo_ready = sem("h2t_lo_ready")
    qk_in_psum = sem("qk_in_psum")
    qk_hi_ready = sem("qk_hi_ready")
    qk_lo_ready = sem("qk_lo_ready")
    v_in_psum = sem("v_in_psum")
    v1_ready = sem("v1_ready")
    v_rest_ready = sem("v_rest_ready")
    v2_ready = sem("v2_ready")
    v3_ready = sem("v3_ready")
    scores_in_psum = sem("scores_in_psum")
    biased_ready = sem("biased_ready")
    nonzero_ready = sem("nonzero_ready")
    exp_ready = sem("exp_ready")
    p_hi_ready = sem("p_hi_ready")
    p_lo_ready = sem("p_lo_ready")
    pt_in_psum = sem("pt_in_psum")
    pt_ready = sem("pt_ready")
    pv_in_psum = sem("pv_in_psum")
    o_raw_ready = sem("o_raw_ready")
    row_scale_ready = sem("row_scale_ready")
    o_ready = sem("o_ready")
    ot_in_psum = sem("ot_in_psum")
    ot_hi_ready = sem("ot_hi_ready")
    ot_lo_ready = sem("ot_lo_ready")
    projected = sem("projected")
    result_ready = sem("result_ready")
    stored = [sem(f"stored{u}") for u in range(2)]

    def head_at(i, u, h, last):
        if h < 0 or (h >= H and last):
            return None
        if h < H:
            return i, u, h
        return (i, 1, h - H) if u == 0 else (i + 1, 0, h - H)

    def nxt(i, u):
        return (i, 1) if u == 0 else (i + 1, 0)

    def run(eng, slot):
        def pair(i, last):
            for u in range(2):
                for s in range(FIRST, FIRST + H):
                    slot(i, u, s, last and u == 1, last)

        for s in range(-LEAD, FIRST):
            slot(0, 0, s, False, False)
        pair(0, False)
        with eng.Fori(1, PAIRS - 1) as i:
            pair(i, False)
        pair(PAIRS - 1, True)

    block = ctx.enter_context(nc.Block())

    @block.sync
    def _(sp):
        def load(i, u):
            b = 2 * i + u
            sp.dma_start(y[:, u].rearrange("p k n -> p (k n)"), scratch[b]).then_inc(landed[u], 16)
            sp.dma_start(x_in[:, u], x_rows[b]).then_inc(landed[u], 16)

        def load_adj(i, u):
            sp.dma_start(adj_in[:], adj_rows[2 * i + u]).then_inc(adj_landed, 16)

        load(0, 0)
        load_adj(0, 0)
        load(0, 1)
        sp.wait_ge(bias_ready, 1)
        load_adj(0, 1)

        def pair(i, last):
            for u in range(2):
                b = 2 * i + u
                if not last:
                    sp.wait_ge(x1_ready, NT * (b + 1))
                    load(i + 1, u)
                    sp.wait_ge(bias_ready, b + 2)
                    load_adj(i + 1, u)
                for t in range(NT):
                    sp.wait_ge(result_ready, NT * b + t + 1)
                    sp.dma_start(out_rows[b][:, t], result[:, u, t]).then_inc(stored[u], 16)

        pair(0, False)
        with sp.Fori(1, PAIRS - 1) as i:
            pair(i, False)
        pair(PAIRS - 1, True)
        for u in range(2):
            sp.wait_ge(stored[u], 16 * NT * PAIRS)

    @block.gpsimd
    def _(pool):
        def double_adj(i, u):
            b = 2 * i + u
            pool.wait_ge(adj_landed, 16 * (b + 1))
            pool.tensor_tensor(bias[:, u], adj_in[:], adj_in[:], ALU.add).then_inc(bias_ready, 1)

        def apply_bn(i, u):
            b = 2 * i + u
            wait_past(pool, y_ready, b)
            pool.tensor_copy(scale_shift[:], bn_apply[:, :, bass.ds(b, 1)].rearrange("p s o k -> p s (o k)")
                             ).then_inc(scale_shift_ready, 1)
            wait_alone(pool, scale_shift_ready, b + 1)
            wait_alone(pool, landed[u], 32 * (i + 1))
            for k in range(KT):
                op = pool.tensor_scalar(y[:, u, k], y[:, u, k], scale_shift[:, 0, k:k + 1], scale_shift[:, 1, k:k + 1],
                                        ALU.mult, ALU.add)
            op.then_inc(y_ready, 1)

        def normaliser(i, u):
            b = 2 * i + u
            wait_past(pool, ln_ready, b)
            wait_alone(pool, moments_ready, b + 1)
            pool.tensor_scalar(ln_tmp[:, 0], moments[:, :, 1], LN_EPS, 1.0, ALU.add, ALU.mult)
            pool.tensor_scalar(ln_tmp[:, 1], moments[:, :, 0], -1.0, 1.0, ALU.mult, ALU.mult).then_inc(pool_step, 1)
            pool.wait_ge(pool_step, 2 * b + 1)
            pool.tensor_tensor(ln_scale[:], ln_tmp[:, 0], neg_half[:], ALU.pow).then_inc(pool_step, 1)
            pool.wait_ge(pool_step, 2 * b + 2)
            pool.tensor_tensor(ln_shift[:], ln_tmp[:, 1], ln_scale[:], ALU.mult).then_inc(ln_ready, 1)

        def split_v(i, u, t):
            n = NT * (2 * i + u) + t + 1
            rest = v_rest[:, t].rearrange("p (h d) -> p h d", h=H)
            wait_alone(pool, v_rest_ready, n)
            pool.tensor_copy(v[:, u, t, :, HD:2 * HD], rest).then_inc(v2_ready, 1)
            pool.wait_ge(v2_ready, n)
            pool.tensor_tensor(v[:, u, t, :, 2 * HD:3 * HD], rest, v[:, u, t, :, HD:2 * HD],
                               ALU.subtract).then_inc(v3_ready, 1)

        def split_prob(i, u, h):
            g = H * (2 * i + u) + h
            wait_past(pool, pt_in_psum, g - 3)
            wait_alone(pool, exp_ready, g + 1)
            pool.tensor_scalar(prob16[:, h % 4, 0], prob[:, h % 4], 1.0, 1.0, ALU.mult, ALU.mult).then_inc(p_hi_ready, 1)
            pool.wait_ge(p_hi_ready, g + 1)
            pool.tensor_tensor(prob16[:, h % 4, 1], prob[:, h % 4], prob16[:, h % 4, 0], ALU.subtract).then_inc(p_lo_ready, 1)

        double_adj(0, 0)
        apply_bn(0, 0)
        double_adj(0, 1)
        apply_bn(0, 1)
        for u in range(2):
            pool.memset(v[:, u, :, :, 3 * HD:3 * HD + 1], 1.0)
            op = pool.memset(v[:, u, :, :, 3 * HD + 1:VW], 0.0)
        op.then_inc(ones_ready, 1)
        normaliser(0, 0)
        split_v(0, 0, 0)
        split_v(0, 0, 1)

        def slot(i, u, s, last, last_pair):
            ni, nu = nxt(i, u)
            if s == AT_Y + 1 and not last:
                normaliser(ni, nu)
            if not last:
                for t in range(NT):
                    if s == AT_V[t][1] + 1:
                        split_v(ni, nu, t)
            if s == AT_BIAS and not last_pair:
                pool.wait_ge(biased_ready, H * (2 * i + u + 1))
                double_adj(i + 1, u)
            if s == AT_APPLY and not last_pair:
                apply_bn(i + 1, u)
            if head := head_at(i, u, s + LEAD, last):
                split_prob(*head)

        run(pool, slot)

    @block.scalar
    def _(act):
        def normalise(i, u):
            b = 2 * i + u
            wait_past(act, h2t_in_psum, b)
            act.wait_ge(ln_ready, b + 1)
            for t in range(NT):
                op = act.activation(h2[:, t], x1[:, u, t], ACT.Relu, bias=ln_shift[:, t:t + 1], scale=ln_scale[:, t:t + 1])
            op.then_inc(h2_ready, 1)

        def h2t_high(i, u):
            act.wait_ge(h2t_in_psum, 2 * i + u + 1)
            for half in range(2):
                act.activation(h2t[:, 0, 2 * half:2 * half + 2], ps_g[:, half], ACT.Copy).then_inc(h2t_hi_ready, 1)

        def qk_high(i, u, t):
            act.wait_ge(qk_in_psum, KT * (2 * i + u) + t + 1)
            act.activation(q[:, u, 0, t], ps_g[:, t % 2, 0:N], ACT.Copy, scale=SCALE)
            act.activation(k_[:, u, 0, t], ps_g[:, t % 2, N:2 * N], ACT.Copy).then_inc(qk_hi_ready, 1)

        def v_high(i, u, t):
            act.wait_ge(v_in_psum, NT * (2 * i + u) + t + 1)
            act.activation(v[:, u, t, :, 0:HD], ps_g[:, 1 - t].rearrange("p (h d) -> p h d", h=H), ACT.Copy).then_inc(v1_ready, 1)

        def ot_high(i, u):
            b = 2 * i + u
            wait_past(act, projected, NT * b)
            act.wait_ge(ot_in_psum, b + 1)
            for half in range(2):
                act.activation(ot[:, 0, 2 * half:2 * half + 2], ps_g[:, half], ACT.Copy).then_inc(ot_hi_ready, 1)

        def softmax_exp(i, u, h):
            g = H * (2 * i + u) + h
            wait_past(act, p_lo_ready, g - 3)
            act.wait_ge(biased_ready, g + 1)
            for t in range(NT):
                op = act.activation(prob[:, h % 4, t], a[:, h % 2, t], ACT.Exp, bias=least[:, h % 4, t:t + 1], scale=-1.0)
            op.then_inc(exp_ready, 1)

        def pt_out(i, u, h):
            g = H * (2 * i + u) + h
            wait_past(act, pv_in_psum, g - 1)
            act.wait_ge(pt_in_psum, g + 1)
            act.activation(pt[:, h % 2], ps_pt[:, h % 2], ACT.Copy).then_inc(pt_ready, 1)

        normalise(0, 0)
        h2t_high(0, 0)
        qk_high(0, 0, 0)
        v_high(0, 0, 0)
        v_high(0, 0, 1)
        qk_high(0, 0, 1)
        qk_high(0, 0, 2)

        def slot(i, u, s, last, last_pair):
            ni, nu = nxt(i, u)
            if head := head_at(i, u, s + LEAD, last):
                softmax_exp(*head)
            if s == AT_QK3[1]:
                qk_high(i, u, 3)
            if not last:
                if s == AT_H:
                    h2t_high(ni, nu)
                for t, at in AT_QK.items():
                    if s == at[1]:
                        qk_high(ni, nu, t)
                for t, at in AT_V.items():
                    if s == at[1]:
                        v_high(ni, nu, t)
            if s == AT_O:
                ot_high(i, u)
            if head := head_at(i, u, s + 1, last):
                pt_out(*head)
            if s == AT_NORM and not last:
                normalise(ni, nu)

        run(act, slot)

    @block.vector
    def _(dve):
        def residual_one(i, u):
            b = 2 * i + u
            dve.wait_ge(landed[u], 32 * (i + 1))
            dve.wait_ge(y_in_psum, b + 1)
            for t in range(NT):
                dve.scalar_tensor_tensor(out=x1[:, u, t], in0=ps_g[:, t], scalar=0.0, in1=x_in[:, u, t],
                                         op0=ALU.max, op1=ALU.add).then_inc(x1_ready, 1)
            wait_past(dve, moments_ready, b)
            wait_past(dve, ln_ready, b)
            dve.wait_ge(x1_ready, NT * (b + 1))
            for t in range(NT):
                op = dve.bn_stats(partials[:, t], x1[:, u, t])
            op.then_inc(partials_ready, 1)
            wait_alone(dve, partials_ready, b + 1)
            for t in range(NT):
                op = dve.bn_aggr(moments[:, t], partials[:, t])
            op.then_inc(moments_ready, 1)

        def h2t_low(i, u):
            for half in range(2):
                dve.wait_ge(h2t_hi_ready, 2 * (2 * i + u) + half + 1)
                dve.tensor_tensor(h2t[:, 1, 2 * half:2 * half + 2].rearrange("p k n -> p (k n)"), ps_g[:, half],
                                  h2t[:, 0, 2 * half:2 * half + 2].rearrange("p k n -> p (k n)").bitcast(F32),
                                  ALU.subtract).then_inc(h2t_lo_ready, 1)

        def qk_low(i, u, t):
            dve.wait_ge(qk_hi_ready, KT * (2 * i + u) + t + 1)
            dve.scalar_tensor_tensor(out=q[:, u, 1, t], in0=ps_g[:, t % 2, 0:N], scalar=SCALE,
                                     in1=q[:, u, 0, t].bitcast(F32), op0=ALU.mult, op1=ALU.subtract)
            dve.tensor_tensor(k_[:, u, 1, t], ps_g[:, t % 2, N:2 * N], k_[:, u, 0, t].bitcast(F32),
                              ALU.subtract).then_inc(qk_lo_ready, 1)

        def v_remainder(i, u, t):
            dve.wait_ge(v1_ready, NT * (2 * i + u) + t + 1)
            dve.tensor_tensor(v_rest[:, t].rearrange("p (h d) -> p h d", h=H), ps_g[:, 1 - t].rearrange("p (h d) -> p h d", h=H),
                              v[:, u, t, :, 0:HD], ALU.subtract).then_inc(v_rest_ready, 1)

        def add_bias(i, u, h):
            g = H * (2 * i + u) + h
            wait_past(dve, exp_ready, g - 1)
            wait_past(dve, nonzero_ready, g - 1)
            if h == 0:
                dve.wait_ge(bias_ready, 2 * i + u + 1)
            wait_alone(dve, scores_in_psum, g + 1)
            for t in range(NT):
                op = dve.tensor_tensor_reduce(a[:, h % 2, t], ps_s[:, h % 2, t], bias[:, u, t], -1.0, BIG,
                                              ALU.add, ALU.min, least[:, h % 4, t:t + 1])
            op.then_inc(biased_ready, 1)
            dve.wait_ge(biased_ready, g + 1)
            dve.tensor_reduce(nonzero[:, u, :, h], a[:, h % 2], AX_X, ALU.max,
                              apply_absolute_value=True).then_inc(nonzero_ready, 1)

        def gather_quad(i, u, c):
            n = 4 * (2 * i + u) + c
            dve.wait_ge(pv_in_psum, 4 * (n + 1))
            wait_past(dve, o_ready, n)
            for t in range(NT):
                heads = ps_o[:, t, 0:4 * VW].rearrange("p (h w) -> p h w", h=4)
                dve.tensor_reduce(o_raw[:, t], heads[:, :, 0:3 * HD].rearrange("p h (c d) -> p h d c", c=3), AX_X, ALU.add)
                op = dve.reciprocal(row_sum[:, t], heads[:, :, 3 * HD])
            op.then_inc(o_raw_ready, 1)
            dve.wait_ge(o_raw_ready, n + 1)
            dve.scalar_tensor_tensor(out=row_scale[:], in0=nonzero[:, u, :, 4 * c:4 * c + 4], scalar=0.0, in1=row_sum[:],
                                     op0=ALU.is_gt, op1=ALU.mult).then_inc(row_scale_ready, 1)
            dve.wait_ge(row_scale_ready, n + 1)
            if c == 0:
                wait_past(dve, ot_in_psum, 2 * i + u)
            dve.tensor_tensor(o[:, :, 4 * c:4 * c + 4], o_raw[:], row_scale[:].unsqueeze(3).to_broadcast([P, NT, 4, HD]),
                              ALU.mult).then_inc(o_ready, 1)

        def ot_low(i, u):
            for half in range(2):
                dve.wait_ge(ot_hi_ready, 2 * (2 * i + u) + half + 1)
                dve.tensor_tensor(ot[:, 1, 2 * half:2 * half + 2].rearrange("p k n -> p (k n)"), ps_g[:, half],
                                  ot[:, 0, 2 * half:2 * half + 2].rearrange("p k n -> p (k n)").bitcast(F32),
                                  ALU.subtract).then_inc(ot_lo_ready, 1)

        def residual_two(i, u, t):
            wait_past(dve, stored[u], 16 * NT * i)
            dve.wait_ge(projected, NT * (2 * i + u) + t + 1)
            dve.tensor_tensor(result[:, u, t], ps_g[:, t], x1[:, u, t], ALU.add).then_inc(result_ready, 1)

        residual_one(0, 0)
        h2t_low(0, 0)
        qk_low(0, 0, 0)
        v_remainder(0, 0, 0)
        v_remainder(0, 0, 1)
        qk_low(0, 0, 1)
        qk_low(0, 0, 2)

        def slot(i, u, s, last, last_pair):
            ni, nu = nxt(i, u)
            if head := head_at(i, u, s + LEAD, last):
                add_bias(*head)
            if s == AT_QK3[1]:
                qk_low(i, u, 3)
            if not last:
                if s == AT_Y:
                    residual_one(ni, nu)
                if s == AT_H:
                    h2t_low(ni, nu)
                for t, at in AT_QK.items():
                    if s == at[1]:
                        qk_low(ni, nu, t)
                for t, at in AT_V.items():
                    if s == at[1]:
                        v_remainder(ni, nu, t)
            if s == AT_O:
                ot_low(i, u)
            if s in AT_PROJECT:
                residual_two(i, u, AT_PROJECT[s])
            if (head := head_at(i, u, s, last)) and head[2] % 4 == 3:
                gather_quad(head[0], head[1], head[2] // 4)

        run(dve, slot)

    @block.tensor
    def _(pe):
        def y_back(i, u):
            b = 2 * i + u
            wait_past(pe, result_ready, NT * (b - 1))
            pe.wait_ge(y_ready, b + 1)
            for t in range(NT):
                for k in range(KT):
                    op = pe.transpose(ps_g[:, t, k * P:(k + 1) * P], y[:, u, k, t * P:(t + 1) * P], ident[:])
            op.then_inc(y_in_psum, 1)

        def transpose_h2(i, u):
            b = 2 * i + u
            wait_past(pe, qk_lo_ready, KT * b)
            pe.wait_ge(h2_ready, b + 1)
            for k in range(KT):
                for t in range(NT):
                    c = k % 2 * N + t * P
                    op = pe.transpose(ps_g[:, k // 2, c:c + P], h2[:, t, k * P:(k + 1) * P], ident[:])
            op.then_inc(h2t_in_psum, 1)

        def project_qk(i, u, t, w):
            b = 2 * i + u
            if w == 0:
                if t == 0:
                    pe.wait_ge(h2t_lo_ready, 2 * (b + 1))
                else:
                    pe.wait_ge(v_rest_ready, NT * b + t)
            for n, (s, m) in enumerate(HILO):
                for k in range(KT):
                    weights = (attn_hi, attn_lo)[s]
                    op = pe.matmul(ps_g[:, t % 2, w * N:(w + 1) * N], weights[:, w * KT + k, t * P:(t + 1) * P],
                                   h2t[:, m, k], start=(n == 0 and k == 0), stop=(n == 2 and k == KT - 1))
            if w == 1:
                op.then_inc(qk_in_psum, 1)

        def last_qk(i, u, w, last):
            if w == 0:
                if last:
                    pe.wait_ge(result_ready, NT * (2 * i + u))
                else:
                    pe.wait_ge(x1_ready, NT * (2 * i + u + 2))
            project_last(i, u, w)

        def project_last(i, u, w):
            t = KT - 1
            for n, (s, m) in enumerate(HILO):
                for k in range(KT):
                    weights = (attn_hi, attn_lo)[s]
                    op = pe.matmul(ps_g[:, t % 2, w * N:(w + 1) * N], weights[:, w * KT + k, t * P:(t + 1) * P],
                                   h2t[:, m, k], start=(n == 0 and k == 0), stop=(n == 2 and k == KT - 1))
            if w == 1:
                op.then_inc(qk_in_psum, 1)

        def project_v(i, u, t, products):
            if products[0] == 0 and t == 1:
                pe.wait_ge(qk_lo_ready, KT * (2 * i + u) + 1)
            for n in products:
                s, m = HILO[n]
                for k in range(KT):
                    op = pe.matmul(ps_g[:, 1 - t], h2t[:, s, k, t * P:(t + 1) * P], (attn_hi, attn_lo)[m][:, 2 * KT + k],
                                   start=(n == 0 and k == 0), stop=(n == 2 and k == KT - 1))
            if n == 2:
                op.then_inc(v_in_psum, 1)

        def score(i, u, h):
            g = H * (2 * i + u) + h
            wait_past(pe, biased_ready, g - 1)
            pe.wait_ge(qk_lo_ready, KT * (2 * i + u) + h // HPT + 1)
            rows = slice(h % HPT * HD, h % HPT * HD + HD)
            for t in range(NT):
                for n, (s, m) in enumerate(HILO):
                    op = pe.matmul(ps_s[:, h % 2, t], q[rows, u, s, h // HPT, t * P:(t + 1) * P], k_[rows, u, m, h // HPT],
                                   start=(n == 0), stop=(n == 2))
            op.then_inc(scores_in_psum, 1)

        def transpose_prob(i, u, h):
            g = H * (2 * i + u) + h
            wait_past(pe, pt_ready, g - 1)
            pe.wait_ge(p_lo_ready, g + 1)
            for part in range(2):
                for m in range(NT):
                    for t in range(NT):
                        op = pe.transpose(ps_pt[:, h % 2, part, m, t * P:(t + 1) * P],
                                          prob16[:, h % 4, part, t, m * P:(m + 1) * P], ident16[:])
            op.then_inc(pt_in_psum, 1)

        def times_v(i, u, h):
            b = 2 * i + u
            g = H * b + h
            if h == 0:
                pe.wait_ge(v3_ready, NT * (b + 1))
            if h % 4 == 0:
                wait_past(pe, o_raw_ready, 4 * b + h // 4)
            pe.wait_ge(pt_ready, g + 1)
            c = h % 4 * VW
            for t in range(NT):
                for n, (part, m) in enumerate([(part, m) for part in range(2) for m in range(NT)]):
                    op = pe.matmul(ps_o[:, t, c:c + VW], pt[:, h % 2, part, m, t * P:(t + 1) * P], v[:, u, m, h],
                                   start=(n == 0), stop=(n == 3))
            op.then_inc(pv_in_psum, 1)

        def transpose_o(i, u, last):
            b = 2 * i + u
            pe.wait_ge(qk_lo_ready, KT * (b + 1) + (0 if last else 3))
            pe.wait_ge(o_ready, 4 * (b + 1))
            flat = o[:].rearrange("p t h d -> p t (h d)")
            for k in range(KT):
                for t in range(NT):
                    c = k % 2 * N + t * P
                    op = pe.transpose(ps_g[:, k // 2, c:c + P], flat[:, t, k * P:(k + 1) * P], ident[:])
            op.then_inc(ot_in_psum, 1)

        def project_o(i, u, t):
            pe.wait_ge(ot_lo_ready, 2 * (2 * i + u + 1))
            for n, (s, m) in enumerate(HILO):
                for k in range(KT):
                    op = pe.matmul(ps_g[:, t], ot[:, s, k, t * P:(t + 1) * P], (attn_hi, attn_lo)[m][:, 3 * KT + k],
                                   start=(n == 0 and k == 0), stop=(n == 2 and k == KT - 1))
            op.then_inc(projected, 1)

        y_back(0, 0)
        transpose_h2(0, 0)
        for w in range(2):
            project_qk(0, 0, 0, w)
        pe.wait_ge(ones_ready, 1)
        project_v(0, 0, 0, (0, 1, 2))
        project_v(0, 0, 1, (0, 1, 2))
        for t in (1, 2):
            for w in range(2):
                project_qk(0, 0, t, w)

        def slot(i, u, s, last, last_pair):
            ni, nu = nxt(i, u)
            if head := head_at(i, u, s + LEAD, last):
                score(*head)
            if s in AT_QK3:
                last_qk(i, u, AT_QK3.index(s), last)
            if not last:
                if s == AT_Y:
                    y_back(ni, nu)
                if s == AT_H:
                    transpose_h2(ni, nu)
                for t, at in AT_QK.items():
                    if s in at:
                        project_qk(ni, nu, t, at.index(s))
                for t, at in AT_V.items():
                    if at[0] == at[1] == s:
                        project_v(ni, nu, t, (0, 1, 2))
                    elif s in at:
                        project_v(ni, nu, t, ((0,), (1, 2))[at.index(s)])
            if s == AT_O:
                transpose_o(i, u, last)
            if s in AT_PROJECT:
                project_o(i, u, AT_PROJECT[s])
            if head := head_at(i, u, s + 1, last):
                transpose_prob(*head)
            if head := head_at(i, u, s, last):
                times_v(*head)

        run(pe, slot)


def kernel(**inputs):
    import numpy as np
    import concourse.bacc as bacc
    from concourse.bass_utils import run_bass_kernel_spmd

    def tiled(a):
        return a.reshape(E, KT, P).transpose(2, 0, 1)

    arrays = {
        "x": inputs["x"],
        "adj": inputs["adj"],
        "adj_t": inputs["adj"].transpose(0, 2, 1),
        "router_w": inputs["L0_gnn_router_w"],
        "router_b": inputs["L0_gnn_router_b"].reshape(1, E),
        "expert_w": inputs["L0_gnn_expert_w"],
        "gamma": tiled(inputs["L0_gnn_bn_gamma"]),
        "beta": tiled(inputs["L0_gnn_bn_beta"]),
        "attn_w": np.stack([inputs[f"L1_gnn_W{c}"].T for c in "qkvo"]),
    }
    arrays = {f"in_{name}": np.ascontiguousarray(a) for name, a in arrays.items()}
    nc = bacc.Bacc("TRN2", target_bir_lowering=False, num_devices=1)
    args = [nc.dram_tensor(name, a.shape, mybir.dt.from_np(a.dtype), kind="ExternalInput").ap() for name, a in arrays.items()]
    out = nc.dram_tensor("out", (B, N, D), F32, kind="ExternalOutput").ap()
    build(nc, *args, out)
    return run_bass_kernel_spmd(nc, [arrays], core_ids=[0]).results[0]["out"]
```

```python
from contextlib import ExitStack

import concourse.bass as bass
from concourse import mybir

F32 = mybir.dt.float32
F32R = mybir.dt.float32r
BF16 = mybir.dt.bfloat16
F16 = mybir.dt.float16
U32 = mybir.dt.uint32
ALU = mybir.AluOpType
ACT = mybir.ActivationFunctionType
AX_X = mybir.AxisListType.X

P = 128
B = 32
N = 256
D = 512
E = 4
H = 16
HD = D // H
NT = N // P
KT = D // P
HPT = P // HD
PAIRS = B // 2
SCALE = float(D) ** -0.5
LN_EPS = 1e-5
BN_EPS = 1e-5
BIG = 3.0e38
HALF = KT // 2
VW = 3 * HD + 2
LEAD = 4
FIRST = 4

SUPPORT_PIECES = ((0, slice(0, D)), (1, slice(0, D // 2)), (1, slice(D // 2, D)))
SP = len(SUPPORT_PIECES)

HILO = ((0, 0), (0, 1), (1, 0))


def build(nc, x, adj, adj_t, router_w, router_b, expert_w, gamma, beta, attn_w, out):
    with ExitStack() as ctx:
        def sem(name):
            return ctx.enter_context(nc.semaphore(name))

        scratch = nc.dram_tensor("out_t_scratch", (B, P, KT * N), F32, kind="Internal").ap()
        x_rows = x.rearrange("b (t p) d -> b p t d", p=P)
        out_rows = out.rearrange("b (t p) d -> b p t d", p=P)
        adj_rows = adj.rearrange("b (t p) m -> b p t m", p=P)
        adj_t_rows = adj_t.rearrange("b (t p) n -> b p t n", p=P)
        expert_rows = expert_w.rearrange("e (k p) d -> e p k d", p=P)
        attn_rows = attn_w.rearrange("w (k p) d -> (w k) p d", p=P)

        def sb(name, shape, dt=F32, stack=ctx):
            return stack.enter_context(nc.sbuf_tensor(name, shape, dt))

        attn_hi = sb("attn_hi", [P, 4 * KT, D], F32R)
        with nc.sbuf_tensor("raw_w", [P, E * KT, D], F32) as raw_w:
            pass
        attn_lo = sb("attn_lo", [P, 4 * KT, D], F32R)
        ident = sb("ident", [P, P])
        ident16 = sb("ident16", [P, P], F16)
        neg_half = sb("neg_half", [P, 2])
        out_moments = sb("out_moments", [P, B, KT, 6])
        top1_row = sb("top1_row", [1, B])
        bn_apply = sb("bn_apply", [P, 2, B, KT])
        h = sb("h", [P, 2, NT, D])
        out_t = sb("out_t", [P, 2, KT, N])

        def ps(name, shape, dt=F32, stack=ctx):
            return stack.enter_context(nc.psum_tensor(name, shape, dt))

        ident_zero = sem("ident_zero")
        ident_ready = sem("ident_ready")
        small_landed = sem("small_landed")
        raw_w_landed = [sem(f"raw_w_landed{e}") for e in range(E)]
        expert_hi_ready = sem("expert_hi_ready")
        expert_lo_ready = sem("expert_lo_ready")
        pads_ready = sem("pads_ready")
        x_landed = [sem(f"x_landed{u}") for u in range(2)]
        adj_t_landed = [sem(f"adj_t_landed{u}") for u in range(2)]
        attn_raw_landed = sem("attn_raw_landed")
        attn_hi_ready = sem("attn_hi_ready")
        attn_lo_ready = sem("attn_lo_ready")
        partials_ready = sem("partials_ready")
        moments_ready = sem("moments_ready")
        pool_step = sem("pool_step")
        ln_ready = sem("ln_ready")
        h_ready = sem("h_ready")
        ht_in_psum = sem("ht_in_psum")
        ht_hi_ready = sem("ht_hi_ready")
        ht_lo_ready = sem("ht_lo_ready")
        logits_in_psum = sem("logits_in_psum")
        logits_ready = sem("logits_ready")
        best_ready = sem("best_ready")
        index_ready = sem("index_ready")
        support_in_psum = sem("support_in_psum")
        support_hi_ready = sem("support_hi_ready")
        support_lo_ready = sem("support_lo_ready")
        adj_hi_ready = sem("adj_hi_ready")
        adj_ready = sem("adj_ready")
        out_in_psum = sem("out_in_psum")
        out_t_ready = sem("out_t_ready")
        out_moments_ready = sem("out_moments_ready")
        out_t_stored = [sem(f"out_t_stored{u}") for u in range(2)]
        graph_landed = [sem(f"graph_landed{u}") for u in range(2)]
        top1_ready = sem("top1_ready")
        top1_spread = sem("top1_spread")
        bn_step = sem("bn_step")
        bn_var_ready = sem("bn_var_ready")
        bn_inv_step = sem("bn_inv_step")
        bn_ready = sem("bn_ready")

        def wait_past(eng, which, value):
            if not isinstance(value, int) or value > 0:
                eng.wait_ge(which, value)

        waits_passed = sem("waits_passed")

        def wait_alone(eng, which, value):
            eng.wait_ge(which, value)
            eng.sem_inc(waits_passed, 1)

        with ExitStack() as one:
            expert_hi = sb("expert_hi", [P, E * KT, D], F32R, one)
            expert_lo = sb("expert_lo", [P, E * KT, D], F32R, one)
            attn_raw = sb("attn_raw", [P, D], F32, one)
            router = sb("router", [P, KT, E], F32, one)
            router_bias = sb("router_bias", [1, E], F32, one)
            bn_gb = sb("bn_gb", [P, 2, E, KT], F32, one)
            x_in = sb("x_in", [P, 2, NT, D], F32, one)
            adj_t_in = sb("adj_t_in", [P, 2, NT, N], F32, one)
            adj_t_hl = sb("adj_t_hl", [P, 2, 2, NT, N], F32R, one)
            partials = sb("partials", [P, NT, 6], F32, one)
            moments = sb("moments", [P, 2, NT, 2], F32, one)
            ln_tmp = sb("ln_tmp", [P, 2, NT], F32, one)
            ln_scale = sb("ln_scale", [P, 2, NT], F32, one)
            ln_shift = sb("ln_shift", [P, 2, NT], F32, one)
            ht_hl = sb("ht_hl", [P, 2, 2, KT, N], F32R, one)
            h_sum = sb("h_sum", [P, 2, KT], F32, one)
            logits = sb("logits", [1, 8], F32, one)
            best = sb("best", [1, 8], F32, one)
            index = sb("index", [1, 2, 8], U32, one)
            support_hl = sb("support_hl", [P, 2, NT, D], F32R, one)
            ones_row = sb("ones_row", [1, P], F32, one)
            x_flat = x_in[:].rearrange("p u t d -> p (u t d)")
            taken = [0]

            def tmp(*shape):
                size = 1
                for s in shape:
                    size *= s
                taken[0] += size
                names = " ".join("abcd"[:len(shape)])
                return x_flat[:, taken[0] - size:taken[0]].rearrange(f"p ({names}) -> p {names}", **dict(zip("abcd", shape)))

            top1_all = tmp(B)
            onehot = tmp(E, B)
            gsum = tmp(2, KT, B)
            pick = tmp(E, KT, B)
            gtmp = tmp(2, KT, B)
            esum = tmp(2, E, KT)
            ecount = tmp(E)
            emean = tmp(2, E, KT)
            evar = tmp(E, KT)
            einv = tmp(E, KT)
            eab = tmp(2, E, KT)
            etmp = tmp(E, KT)
            bn_half = sb("bn_half", [P, E, KT], F32, one)
            ps_ht = ps("ps_ht", [P, KT, N], F32, one)
            ps_support = ps("ps_support", [P, NT, D], F32, one)
            ps_out = ps("ps_out", [P, KT, N], F32, one)
            ps_small = ps("ps_small", [P, 512], F32, one)

            block = one.enter_context(nc.Block())

            @block.sync
            def _(sp):
                def load_x(i, u):
                    sp.dma_start(x_in[:, u], x_rows[2 * i + u]).then_inc(x_landed[u], 16)

                def load_adj(i, u):
                    sp.dma_start(adj_t_in[:, u], adj_t_rows[2 * i + u]).then_inc(adj_t_landed[u], 16)

                load_x(0, 0)
                sp.dma_start(raw_w[:, 0:KT], expert_rows[0]).then_inc(raw_w_landed[0], 16)
                sp.dma_start(router[:], router_w.rearrange("(k p) e -> p k e", p=P)).then_inc(small_landed, 16)
                sp.dma_start(router_bias[:], router_b).then_inc(small_landed, 16)
                sp.dma_start(bn_gb[:, 0], gamma).then_inc(small_landed, 16)
                sp.dma_start(bn_gb[:, 1], beta).then_inc(small_landed, 16)
                load_x(0, 1)
                for e in range(1, E):
                    sp.dma_start(raw_w[:, KT * e:KT * (e + 1)], expert_rows[e]).then_inc(raw_w_landed[e], 16)
                load_adj(0, 0)
                load_adj(0, 1)
                sp.wait_ge(h_ready, 1)
                load_x(1, 0)
                sp.wait_ge(expert_lo_ready, KT * E)

                def pair(i, last):
                    wait_past(sp, attn_lo_ready, i)
                    sp.dma_start(attn_raw[:], attn_rows[i]).then_inc(attn_raw_landed, 16)
                    for u in range(2):
                        b = 2 * i + u
                        if not last:
                            sp.wait_ge(adj_ready, b + 1)
                            load_adj(i + 1, u)
                        if not last and u == 0:
                            sp.wait_ge(h_ready, b + 2)
                            load_x(i + 1, 1)
                        if u == 1 and (not isinstance(i, int) or i < PAIRS - 2):
                            sp.wait_ge(h_ready, b + 2)
                            load_x(i + 2, 0)
                        sp.wait_ge(out_t_ready, b + 1)
                        sp.dma_start(scratch[b], out_t[:, u].rearrange("p k n -> p (k n)")).then_inc(out_t_stored[u], 16)

                pair(0, False)
                with sp.Fori(1, PAIRS - 2) as i:
                    pair(i, False)
                pair(PAIRS - 2, False)
                pair(PAIRS - 1, True)
                for u in range(2):
                    sp.wait_ge(out_t_stored[u], 16 * PAIRS)
                for u in range(2):
                    sp.wait_ge(ht_in_psum, B - 1 + u)
                    sp.dma_start(h[:, u], x_rows[u]).then_inc(graph_landed[u], 16)
                for u in range(2):
                    sp.wait_ge(out_moments_ready, B - 1 + u)
                    sp.dma_start(out_t[:, u].rearrange("p k n -> p (k n)"), scratch[u]).then_inc(graph_landed[u], 16)

            @block.gpsimd
            def _(pool):
                pool.memset(ident[:], 0.0)
                pool.memset(ident16[:], 0.0)
                pool.memset(neg_half[:], -0.5)
                pool.memset(bn_half[:], -0.5).then_inc(ident_zero, 1)
                pool.wait_ge(ident_zero, 1)
                for m in (ident, ident16):
                    last_op = pool.affine_select(out=m[:], in_=m[:], compare_op=ALU.not_equal, fill=1.0, base=0,
                                                 pattern=[[-1, P]], channel_multiplier=1)
                last_op.then_inc(ident_ready, 1)

                def normaliser(i, u):
                    b = 2 * i + u
                    wait_past(pool, ln_ready, b)
                    wait_alone(pool, moments_ready, b + 1)
                    pool.tensor_scalar(ln_tmp[:, 0], moments[:, u, :, 1], LN_EPS, 1.0, ALU.add, ALU.mult)
                    pool.tensor_scalar(ln_tmp[:, 1], moments[:, u, :, 0], -1.0, 1.0, ALU.mult, ALU.mult).then_inc(pool_step, 1)
                    pool.wait_ge(pool_step, 2 * b + 1)
                    pool.tensor_tensor(ln_scale[:, u], ln_tmp[:, 0], neg_half[:], ALU.pow).then_inc(pool_step, 1)
                    pool.wait_ge(pool_step, 2 * b + 2)
                    pool.tensor_tensor(ln_shift[:, u], ln_tmp[:, 1], ln_scale[:, u], ALU.mult).then_inc(ln_ready, 1)

                def split_adj(i, u):
                    b = 2 * i + u
                    wait_alone(pool, adj_t_landed[u], 16 * (i + 1))
                    pool.tensor_copy(adj_t_hl[:, u, 0], adj_t_in[:, u]).then_inc(adj_hi_ready, 1)
                    pool.wait_ge(adj_hi_ready, b + 1)
                    pool.tensor_tensor(adj_t_hl[:, u, 1], adj_t_in[:, u], adj_t_hl[:, u, 0].bitcast(F32),
                                       ALU.subtract).then_inc(adj_ready, 1)

                def split_attn(i):
                    wait_alone(pool, attn_raw_landed, 16 * (i + 1))
                    pool.tensor_copy(attn_hi[:, i], attn_raw[:]).then_inc(attn_hi_ready, 1)
                    pool.wait_ge(attn_hi_ready, i + 1)
                    pool.tensor_tensor(attn_lo[:, i], attn_raw[:], attn_hi[:, i].bitcast(F32),
                                       ALU.subtract).then_inc(attn_lo_ready, 1)

                normaliser(0, 0)
                normaliser(0, 1)
                split_adj(0, 0)
                split_adj(0, 1)

                def pair(i, last):
                    for u in range(2):
                        b = 2 * i + u
                        if not last:
                            normaliser(i + 1, u)
                        if u == 0:
                            split_attn(i)
                        if not last:
                            wait_alone(pool, out_in_psum, b + 1)
                            split_adj(i + 1, u)

                pair(0, False)
                with pool.Fori(1, PAIRS - 1) as i:
                    pair(i, False)
                pair(PAIRS - 1, True)

                pool.wait_ge(bn_var_ready, 1)
                pool.tensor_tensor(einv, evar, bn_half[:], ALU.pow).then_inc(bn_inv_step, 1)

            @block.scalar
            def _(act):
                def split_expert(e):
                    act.wait_ge(raw_w_landed[e], 16)
                    for k in range(KT * e, KT * (e + 1)):
                        act.activation(expert_hi[:, k], raw_w[:, k], ACT.Copy).then_inc(expert_hi_ready, 1)

                def normalise(i, u):
                    act.wait_ge(ln_ready, 2 * i + u + 1)
                    for t in range(NT):
                        op = act.activation(h[:, u, t], x_in[:, u, t], ACT.Relu, bias=ln_shift[:, u, t:t + 1],
                                            scale=ln_scale[:, u, t:t + 1])
                    op.then_inc(h_ready, 1)

                def ht_high(i, u):
                    act.wait_ge(ht_in_psum, 2 * i + u + 1)
                    for k in range(KT):
                        act.activation(ht_hl[:, u, 0, k], ps_ht[:, k], ACT.Copy,
                                       accum_out=h_sum[:, u, k:k + 1]).then_inc(ht_hi_ready, 1)

                normalise(0, 0)
                split_expert(0)
                ht_high(0, 0)
                split_expert(1)
                normalise(0, 1)
                for e in range(2, E):
                    split_expert(e)

                def pair(i, last):
                    for u in range(2):
                        b = 2 * i + u
                        ni, nu = (i, 1) if u == 0 else (i + 1, 0)
                        more = u == 0 or not last
                        wait_past(act, out_in_psum, b)
                        for t in range(NT):
                            act.wait_ge(support_in_psum, NT * b + t + 1)
                            act.activation(support_hl[:, 0, t], ps_support[:, t], ACT.Copy).then_inc(support_hi_ready, 1)
                            if t == 0 and more:
                                ht_high(ni, nu)
                        if not last:
                            normalise(i + 1, u)
                        act.wait_ge(out_in_psum, b + 1)
                        wait_past(act, out_t_stored[u], 16 * i)
                        act.activation(out_t[:, u], ps_out[:], ACT.Copy).then_inc(out_t_ready, 1)

                pair(0, False)
                with act.Fori(1, PAIRS - 1) as i:
                    pair(i, False)
                pair(PAIRS - 1, True)

            @block.vector
            def _(dve):
                def row_moments(i, u):
                    wait_past(dve, moments_ready, 2 * i + u)
                    dve.wait_ge(x_landed[u], 16 * (i + 1))
                    for t in range(NT):
                        op = dve.bn_stats(partials[:, t], x_in[:, u, t])
                    op.then_inc(partials_ready, 1)
                    wait_alone(dve, partials_ready, 2 * i + u + 1)
                    for t in range(NT):
                        op = dve.bn_aggr(moments[:, u, t], partials[:, t])
                    op.then_inc(moments_ready, 1)

                def ht_low(i, u):
                    for k in range(0, KT, HALF):
                        dve.wait_ge(ht_hi_ready, KT * (2 * i + u) + k + HALF)
                        dve.tensor_tensor(ht_hl[:, u, 1, k:k + HALF], ps_ht[:, k:k + HALF],
                                          ht_hl[:, u, 0, k:k + HALF].bitcast(F32), ALU.subtract).then_inc(ht_lo_ready, 1)

                def logits_out(i, u):
                    b = 2 * i + u
                    wait_past(dve, index_ready, b)
                    dve.wait_ge(logits_in_psum, b + 1)
                    dve.scalar_tensor_tensor(out=logits[0:1, 0:E], in0=ps_small[0:1, 0:E], scalar=1.0 / N,
                                             in1=router_bias[:], op0=ALU.mult, op1=ALU.add).then_inc(logits_ready, 1)

                def take_best(i, u):
                    b = 2 * i + u
                    wait_alone(dve, logits_ready, b + 1)
                    dve.max(best[:], logits[:]).then_inc(best_ready, 1)

                def take_first(i, u):
                    b = 2 * i + u
                    wait_alone(dve, best_ready, b + 1)
                    dve.max_index(index[:, u], best[:], logits[:]).then_inc(index_ready, 1)
                    dve.wait_ge(index_ready, b + 1)
                    dve.tensor_copy(top1_row[0:1, bass.ds(b, 1)], index[:, u, 0:1]).then_inc(top1_ready, 1)

                step = [0]

                def then(op):
                    step[0] += 1
                    op.then_inc(bn_step, 1)
                    dve.wait_ge(bn_step, step[0])

                def count_graphs():
                    dve.wait_ge(top1_spread, 1)
                    then(dve.tensor_copy(top1_all, ps_small[:, 0:B]))
                    for e in range(E):
                        op = dve.tensor_scalar(onehot[:, e], top1_all, float(e), None, ALU.is_equal)
                    then(op)
                    then(dve.tensor_reduce(ecount, onehot, AX_X, ALU.add))
                    then(dve.tensor_scalar(ecount, ecount, float(N), 1.0, ALU.mult, ALU.max))
                    then(dve.reciprocal(ecount, ecount))

                dve.memset(logits[:], -BIG)
                dve.memset(ones_row[:], 1.0).then_inc(pads_ready, 1)
                dve.wait_ge(pads_ready, 1)
                choice = (logits_out, take_best, take_first)

                def expert_low(e):
                    for k in range(KT * e, KT * (e + 1)):
                        dve.wait_ge(expert_hi_ready, k + 1)
                        dve.tensor_tensor(expert_lo[:, k], raw_w[:, k], expert_hi[:, k].bitcast(F32),
                                          ALU.subtract).then_inc(expert_lo_ready, 1)

                row_moments(0, 0)
                expert_low(0)
                ht_low(0, 0)
                row_moments(0, 1)
                expert_low(1)
                dve.wait_ge(small_landed, 64)
                for step_of_choice in choice:
                    step_of_choice(0, 0)
                for e in range(2, E):
                    expert_low(e)

                def pair(i, last):
                    for u in range(2):
                        b = 2 * i + u
                        ni, nu = (i, 1) if u == 0 else (i + 1, 0)
                        more = u == 0 or not last
                        for n, (t, cols) in enumerate(SUPPORT_PIECES):
                            dve.wait_ge(support_hi_ready, NT * b + t + 1)
                            dve.tensor_tensor(support_hl[:, 1, t, cols], ps_support[:, t, cols],
                                              support_hl[:, 0, t, cols].bitcast(F32), ALU.subtract).then_inc(support_lo_ready, 1)
                            if n == 0 and not last:
                                row_moments(i + 1, u)
                            if n == 0 and more:
                                ht_low(ni, nu)
                            if more:
                                choice[n](ni, nu)
                        if not more:
                            count_graphs()
                        dve.wait_ge(out_t_ready, b + 1)
                        for k in range(KT):
                            op = dve.bn_stats(out_moments[:, b, k], out_t[:, u, k])
                        op.then_inc(out_moments_ready, 1)

                pair(0, False)
                with dve.Fori(1, PAIRS - 1) as i:
                    pair(i, False)
                pair(PAIRS - 1, True)

                dve.wait_ge(out_moments_ready, B)
                m = out_moments[:].rearrange("p b k s -> p s k b")
                half = float(N // 2)
                dve.tensor_tensor(gtmp[:, 0], m[:, 1], m[:, 1], ALU.mult)
                dve.tensor_tensor(gtmp[:, 1], m[:, 4], m[:, 4], ALU.mult)
                then(dve.tensor_tensor(gsum[:, 0], m[:, 1], m[:, 4], ALU.add))
                then(dve.tensor_tensor(gtmp[:, 0], gtmp[:, 0], gtmp[:, 1], ALU.add))
                then(dve.tensor_tensor(gsum[:, 1], m[:, 2], m[:, 5], ALU.add))
                dve.tensor_scalar(gsum[:, 0], gsum[:, 0], half, None, ALU.mult)
                then(dve.scalar_tensor_tensor(out=gsum[:, 1], in0=gtmp[:, 0], scalar=half, in1=gsum[:, 1],
                                              op0=ALU.mult, op1=ALU.add))
                mask = onehot.unsqueeze(2).to_broadcast([P, E, KT, B])
                for s in range(2):
                    then(dve.tensor_tensor(pick, gsum[:, s].unsqueeze(1).to_broadcast([P, E, KT, B]), mask, ALU.mult))
                    then(dve.tensor_reduce(esum[:, s], pick, AX_X, ALU.add))
                for s in range(2):
                    then(dve.tensor_tensor(emean[:, s], esum[:, s], ecount.unsqueeze(2).to_broadcast([P, E, KT]), ALU.mult))
                then(dve.tensor_tensor(etmp, emean[:, 0], emean[:, 0], ALU.mult))
                then(dve.tensor_tensor(evar, emean[:, 1], etmp, ALU.subtract))
                dve.tensor_scalar(evar, evar, BN_EPS, None, ALU.add).then_inc(bn_var_ready, 1)
                dve.wait_ge(bn_inv_step, 1)
                then(dve.tensor_tensor(eab[:, 0], einv, bn_gb[:, 0], ALU.mult))
                then(dve.tensor_tensor(etmp, emean[:, 0], eab[:, 0], ALU.mult))
                then(dve.tensor_tensor(eab[:, 1], bn_gb[:, 1], etmp, ALU.subtract))
                for s in range(2):
                    pv = pick.rearrange("p e k b -> p (e k b)").rearrange("p (b k e) -> p b k e", b=B, k=KT)
                    then(dve.tensor_tensor(pv, onehot.rearrange("p e b -> p b e").unsqueeze(2).to_broadcast([P, B, KT, E]),
                                           eab[:, s].rearrange("p e k -> p k e").unsqueeze(1).to_broadcast([P, B, KT, E]), ALU.mult))
                    then(dve.tensor_reduce(bn_apply[:, s], pv, AX_X, ALU.add))

            @block.tensor
            def _(pe):
                chosen = pe.alloc_register("chosen_expert")

                def transpose_h(i, u):
                    b = 2 * i + u
                    pe.wait_ge(h_ready, b + 1)
                    wait_past(pe, ht_lo_ready, KT // HALF * b)
                    for k in range(KT):
                        for t in range(NT):
                            op = pe.transpose(ps_ht[:, k, t * P:(t + 1) * P], h[:, u, t, k * P:(k + 1) * P], ident[:])
                    op.then_inc(ht_in_psum, 1)

                def take_index(i, u):
                    wait_alone(pe, index_ready, 2 * i + u + 1)
                    pe.reg_load(chosen, index[0:1, u, 0:1])

                def route(i, u):
                    b = 2 * i + u
                    pe.wait_ge(ht_hi_ready, KT * (b + 1))
                    wait_past(pe, index_ready, b)
                    for k in range(KT):
                        op = pe.matmul(ps_small[0:1, 0:E], h_sum[:, u, k:k + 1], router[:, k], start=(k == 0), stop=(k == KT - 1))
                    op.then_inc(logits_in_psum, 1)

                def support(i, u, t, w):
                    b = 2 * i + u
                    wait_past(pe, support_lo_ready, SP * b)
                    for n, (s, m) in enumerate(HILO):
                        if (s, m) == (1, 0):
                            pe.wait_ge(ht_lo_ready, KT // HALF * (b + 1))
                        for k in range(KT):
                            weights = (expert_hi, expert_lo)[m]
                            op = pe.matmul(ps_support[:, t], ht_hl[:, u, s, k, t * P:(t + 1) * P],
                                           weights[:, bass.ds(w + k, 1), :].rearrange("p o d -> p (o d)"),
                                           start=(n == 0 and k == 0), stop=(n == 2 and k == KT - 1))
                    op.then_inc(support_in_psum, 1)

                def aggregate(i, u, tiles):
                    b = 2 * i + u
                    if tiles[0] == 0:
                        pe.wait_ge(adj_ready, b + 1)
                        wait_past(pe, out_t_ready, b)
                    for t in range(NT):
                        for k in tiles:
                            if tiles[0] == 0:
                                pe.wait_ge(support_lo_ready, SP * b + (1 if t == 0 else 2 + k // HALF))
                            for n, (s, m) in enumerate(HILO):
                                op = pe.matmul(ps_out[:, k], support_hl[:, s, t, k * P:(k + 1) * P], adj_t_hl[:, u, m, t],
                                               start=(n == 0 and t == 0), stop=(n == 2 and t == NT - 1))
                    if tiles[0] == 1:
                        op.then_inc(out_in_psum, 1)

                pe.wait_ge(ident_ready, 1)
                transpose_h(0, 0)
                pe.wait_ge(small_landed, 64)
                route(0, 0)
                pe.wait_ge(expert_lo_ready, KT * E)
                take_index(0, 0)

                def pair(i, last):
                    for u in range(2):
                        b = 2 * i + u
                        ni, nu = (i, 1) if u == 0 else (i + 1, 0)
                        more = u == 0 or not last
                        w = pe.snap(chosen, min_val=0, max_val=E - 1) * KT
                        support(i, u, 0, w)
                        if more:
                            transpose_h(ni, nu)
                        support(i, u, 1, w)
                        if more:
                            route(ni, nu)
                        else:
                            pe.wait_ge(top1_ready, B)
                            pe.matmul(ps_small[:, 0:B], ones_row[:], top1_row[:], start=True, stop=True).then_inc(top1_spread, 1)
                        aggregate(i, u, (0, HALF))
                        if more:
                            take_index(ni, nu)
                        aggregate(i, u, (1, HALF + 1))

                pair(0, False)
                with pe.Fori(1, PAIRS - 1) as i:
                    pair(i, False)
                pair(PAIRS - 1, True)

        phase_two(nc, ctx, wait_alone, wait_past, x_rows, adj_rows, scratch, out_rows, attn_hi, attn_lo, ident, ident16,
                  neg_half, bn_apply, h, out_t, graph_landed)


EARLY, MID, LATE = 0.0, 0.25, 0.5
AT_Y = 4 + MID
AT_QK3 = (5 + MID, 6 + MID)
AT_NORM = (5 + LATE, 5 + LATE)
AT_H = (7 + MID, 7 + LATE)
AT_QK = {0: (8 + LATE, 9 + LATE), 1: (13 + LATE, 14 + MID), 2: (15 + MID, 16 + MID)}
AT_V = {0: (10 + MID, 11 + MID), 1: (12 + MID, 12 + MID)}
AT_O = (13 + EARLY, 17 + EARLY)
OUT = {"qk3": (6 + EARLY, 6 + MID), "h0": (6 + MID, 7 + MID), "h1": (7 + EARLY, 7 + MID),
       "qk0": (9 + EARLY, 9 + MID), "v0": (11 + EARLY, 11 + MID), "v1": (12 + EARLY, 12 + MID), "o0": (13 + EARLY, 13 + EARLY),
       "qk1": (14 + EARLY, 14 + MID), "qk2": (16 + EARLY, 16 + MID), "o1": (17 + EARLY, 17 + EARLY)}
FIRST_V = (-4 + MID, -3 + MID)
FIRST_QK = {1: -2 + MID, 2: -1 + MID}
CROWDED = (4, 7)
GATHER_LATER = (5, 7, 9)
AT_PROJECT = {0: (17 + LATE, 18 + MID), 1: (18 + MID, 19 + MID)}
AT_BIAS = 17
AT_APPLY = 18
QK_BANK = (1, 1, 0, 0)
H_BANK = (1, 0)


def phase_two(nc, ctx, wait_alone, wait_past, x_rows, adj_rows, scratch, out_rows, attn_hi, attn_lo, ident, ident16,
              neg_half, bn_apply, x_in, y, landed):
    def sem(name):
        return ctx.enter_context(nc.semaphore(name))

    def sb(name, shape, dt=F32):
        return ctx.enter_context(nc.sbuf_tensor(name, shape, dt))

    def ps(name, shape, dt=F32):
        return ctx.enter_context(nc.psum_tensor(name, shape, dt))

    adj_in = sb("adj_in", [P, NT, N])
    bias = sb("bias", [P, 2, NT, N])
    scale_shift = sb("scale_shift", [P, 2, KT])
    x1 = sb("x1", [P, 2, NT, D])
    partials = sb("partials2", [P, NT, 6])
    moments = sb("moments2", [P, NT, 2])
    ln_tmp = sb("ln_tmp2", [P, 2, NT])
    ln_scale = sb("ln_scale2", [P, NT])
    ln_shift = sb("ln_shift2", [P, NT])
    h2 = sb("h2", [P, NT, D])
    h2t = sb("h2t", [P, 2, KT, N], F32R)
    q = sb("q", [P, 2, 2, KT, N], F32R)
    k_ = sb("k", [P, 2, 2, KT, N], F32R)
    v = sb("v", [P, 2, NT, H, VW], BF16)
    v_rest = sb("v_rest", [P, NT, D])
    a = sb("a", [P, 2, NT, N])
    least = sb("least", [P, 4, NT])
    nonzero = sb("nonzero", [P, 2, NT, H])
    prob = sb("prob", [P, 4, NT, N])
    prob16 = sb("prob16", [P, 4, 2, NT, N], F16)
    pt = sb("pt", [P, 2, 2, NT, N], F16)
    o_raw = sb("o_raw", [P, NT, 2, HD])
    row_sum = sb("row_sum", [P, NT, 2])
    row_scale = sb("row_scale", [P, NT, 2])
    o = sb("o", [P, NT, H, HD])
    ot = sb("ot", [P, 2, KT, N], F32R)
    result = sb("result", [P, 2, NT, D])

    ps_g = ps("ps_g", [P, 2, 512])
    ps_s = ps("ps_s", [P, 2, NT, N])
    ps_pt = ps("ps_pt", [P, 2, 2, NT, N], F16)
    ps_o = ps("ps_o", [P, 2, 512])

    adj_landed = sem("adj_landed")
    ones_ready = sem("ones_ready")
    bias_ready = sem("bias_ready")
    scale_shift_ready = sem("scale_shift_ready")
    y_ready = sem("y_ready")
    y_in_psum = sem("y_in_psum")
    x1_ready = sem("x1_ready")
    partials_ready = sem("partials2_ready")
    moments_ready = sem("moments2_ready")
    pool_step = sem("pool2_step")
    ln_ready = sem("ln2_ready")
    h2_ready = [sem(f"h2_ready{t}") for t in range(NT)]
    h2t_in_psum = sem("h2t_in_psum")
    h2t_hi_ready = sem("h2t_hi_ready")
    h2t_lo_ready = sem("h2t_lo_ready")
    qk_in_psum = sem("qk_in_psum")
    qk_hi_ready = sem("qk_hi_ready")
    qk_lo_ready = sem("qk_lo_ready")
    v_in_psum = sem("v_in_psum")
    v1_ready = sem("v1_ready")
    v_rest_ready = sem("v_rest_ready")
    v2_ready = sem("v2_ready")
    v3_ready = sem("v3_ready")
    scores_in_psum = sem("scores_in_psum")
    biased_ready = sem("biased_ready")
    nonzero_ready = sem("nonzero_ready")
    exp_ready = sem("exp_ready")
    p_hi_ready = sem("p_hi_ready")
    p_lo_ready = sem("p_lo_ready")
    pt_in_psum = sem("pt_in_psum")
    pt_ready = sem("pt_ready")
    pv_in_psum = sem("pv_in_psum")
    o_raw_ready = sem("o_raw_ready")
    row_scale_ready = sem("row_scale_ready")
    o_ready = sem("o_ready")
    ot_in_psum = sem("ot_in_psum")
    ot_hi_ready = sem("ot_hi_ready")
    ot_lo_ready = sem("ot_lo_ready")
    projected = sem("projected")
    result_ready = sem("result_ready")
    stored = [sem(f"stored{u}") for u in range(2)]

    def head_at(i, u, h, last):
        if h < 0 or (h >= H and last):
            return None
        if h < H:
            return i, u, h
        return (i, 1, h - H) if u == 0 else (i + 1, 0, h - H)

    def nxt(i, u):
        return (i, 1) if u == 0 else (i + 1, 0)

    def run(eng, slot):
        def pair(i, last):
            for u in range(2):
                for s in range(FIRST, FIRST + H):
                    slot(i, u, s, last and u == 1, last)

        for s in range(-LEAD, FIRST):
            slot(0, 0, s, False, False)
        pair(0, False)
        with eng.Fori(1, PAIRS - 1) as i:
            pair(i, False)
        pair(PAIRS - 1, True)

    block = ctx.enter_context(nc.Block())

    @block.sync
    def _(sp):
        def load(i, u):
            b = 2 * i + u
            sp.dma_start(y[:, u].rearrange("p k n -> p (k n)"), scratch[b]).then_inc(landed[u], 16)
            sp.dma_start(x_in[:, u], x_rows[b]).then_inc(landed[u], 16)

        def load_adj(i, u):
            sp.dma_start(adj_in[:], adj_rows[2 * i + u]).then_inc(adj_landed, 16)

        load_adj(0, 0)
        sp.wait_ge(bias_ready, 1)
        load_adj(0, 1)

        def pair(i, last):
            for u in range(2):
                b = 2 * i + u
                if not last:
                    sp.wait_ge(x1_ready, NT * (b + 1))
                    load(i + 1, u)
                    sp.wait_ge(bias_ready, b + 2)
                    load_adj(i + 1, u)
                for t in range(NT):
                    sp.wait_ge(result_ready, NT * b + t + 1)
                    sp.dma_start(out_rows[b][:, t], result[:, u, t]).then_inc(stored[u], 16)

        pair(0, False)
        with sp.Fori(1, PAIRS - 1) as i:
            pair(i, False)
        pair(PAIRS - 1, True)
        for u in range(2):
            sp.wait_ge(stored[u], 16 * NT * PAIRS)

    @block.gpsimd
    def _(pool):
        def double_adj(i, u):
            b = 2 * i + u
            pool.wait_ge(adj_landed, 16 * (b + 1))
            pool.tensor_tensor(bias[:, u], adj_in[:], adj_in[:], ALU.add).then_inc(bias_ready, 1)

        def apply_bn(i, u):
            b = 2 * i + u
            wait_past(pool, y_ready, b)
            pool.tensor_copy(scale_shift[:], bn_apply[:, :, bass.ds(b, 1)].rearrange("p s o k -> p s (o k)")
                             ).then_inc(scale_shift_ready, 1)
            wait_alone(pool, scale_shift_ready, b + 1)
            wait_alone(pool, landed[u], 32 * (i + 1))
            for k in range(KT):
                op = pool.tensor_scalar(y[:, u, k], y[:, u, k], scale_shift[:, 0, k:k + 1], scale_shift[:, 1, k:k + 1],
                                        ALU.mult, ALU.add)
            op.then_inc(y_ready, 1)

        def normaliser(i, u):
            b = 2 * i + u
            for t in range(NT):
                wait_past(pool, h2_ready[t], b)
            wait_alone(pool, moments_ready, b + 1)
            pool.tensor_scalar(ln_tmp[:, 0], moments[:, :, 1], LN_EPS, 1.0, ALU.add, ALU.mult)
            pool.tensor_scalar(ln_tmp[:, 1], moments[:, :, 0], -1.0, 1.0, ALU.mult, ALU.mult).then_inc(pool_step, 1)
            pool.wait_ge(pool_step, 2 * b + 1)
            pool.tensor_tensor(ln_scale[:], ln_tmp[:, 0], neg_half[:], ALU.pow).then_inc(pool_step, 1)
            pool.wait_ge(pool_step, 2 * b + 2)
            pool.tensor_tensor(ln_shift[:], ln_tmp[:, 1], ln_scale[:], ALU.mult).then_inc(ln_ready, 1)

        def split_v(i, u, t):
            n = NT * (2 * i + u) + t + 1
            rest = v_rest[:, t].rearrange("p (h d) -> p h d", h=H)
            wait_alone(pool, v_rest_ready, n)
            pool.tensor_copy(v[:, u, t, :, HD:2 * HD], rest).then_inc(v2_ready, 1)
            pool.wait_ge(v2_ready, n)
            pool.tensor_tensor(v[:, u, t, :, 2 * HD:3 * HD], rest, v[:, u, t, :, HD:2 * HD],
                               ALU.subtract).then_inc(v3_ready, 1)

        def split_prob(i, u, h):
            g = H * (2 * i + u) + h
            wait_past(pool, pt_in_psum, g - 3)
            wait_alone(pool, exp_ready, g + 1)
            pool.tensor_scalar(prob16[:, h % 4, 0], prob[:, h % 4], 1.0, 1.0, ALU.mult, ALU.mult).then_inc(p_hi_ready, 1)
            pool.wait_ge(p_hi_ready, g + 1)
            pool.tensor_tensor(prob16[:, h % 4, 1], prob[:, h % 4], prob16[:, h % 4, 0], ALU.subtract).then_inc(p_lo_ready, 1)

        apply_bn(0, 0)
        double_adj(0, 0)
        for u in range(2):
            pool.memset(v[:, u, :, :, 3 * HD:3 * HD + 1], 1.0)
            op = pool.memset(v[:, u, :, :, 3 * HD + 1:VW], 0.0)
        op.then_inc(ones_ready, 1)
        normaliser(0, 0)
        apply_bn(0, 1)
        double_adj(0, 1)

        def slot(i, u, s, last, last_pair):
            ni, nu = nxt(i, u)
            if s - 1 + MID in FIRST_V:
                split_v(i, u, FIRST_V.index(s - 1 + MID))
            if s == AT_Y - MID + 1 and not last:
                normaliser(ni, nu)
            if not last:
                for t in range(NT):
                    if s == AT_V[t][1] - MID + 1:
                        split_v(ni, nu, t)
            if s == AT_BIAS and not last_pair:
                pool.wait_ge(biased_ready, H * (2 * i + u + 1))
                double_adj(i + 1, u)
            if s == AT_APPLY and not last_pair:
                apply_bn(i + 1, u)
            if head := head_at(i, u, s + LEAD, last):
                split_prob(*head)

        run(pool, slot)

    @block.scalar
    def _(act):
        def normalise(i, u):
            b = 2 * i + u
            wait_past(act, h2t_in_psum, 2 * b)
            act.wait_ge(ln_ready, b + 1)
            act.activation(h2[:, 0], x1[:, u, 0], ACT.Relu, bias=ln_shift[:, 0:1], scale=ln_scale[:, 0:1]
                           ).then_inc(h2_ready[0], 1)

        def h2t_high(i, u, half):
            act.wait_ge(h2t_in_psum, 2 * (2 * i + u) + half + 1)
            act.activation(h2t[:, 0, 2 * half:2 * half + 2], ps_g[:, H_BANK[half]], ACT.Relu).then_inc(h2t_hi_ready, 1)

        def qk_high(i, u, t):
            act.wait_ge(qk_in_psum, KT * (2 * i + u) + t + 1)
            act.activation(q[:, u, 0, t], ps_g[:, QK_BANK[t], 0:N], ACT.Copy, scale=SCALE)
            act.activation(k_[:, u, 0, t], ps_g[:, QK_BANK[t], N:2 * N], ACT.Copy).then_inc(qk_hi_ready, 1)

        def v_high(i, u, t):
            act.wait_ge(v_in_psum, NT * (2 * i + u) + t + 1)
            act.activation(v[:, u, t, :, 0:HD], ps_g[:, t].rearrange("p (h d) -> p h d", h=H), ACT.Copy).then_inc(v1_ready, 1)

        def ot_high(i, u, half):
            b = 2 * i + u
            wait_past(act, projected, NT * b)
            act.wait_ge(ot_in_psum, 2 * b + half + 1)
            act.activation(ot[:, 0, 2 * half:2 * half + 2], ps_g[:, half], ACT.Copy).then_inc(ot_hi_ready, 1)

        def softmax_exp(i, u, h):
            g = H * (2 * i + u) + h
            wait_past(act, p_lo_ready, g - 3)
            act.wait_ge(biased_ready, g + 1)
            for t in range(NT):
                op = act.activation(prob[:, h % 4, t], a[:, h % 2, t], ACT.Exp, bias=least[:, h % 4, t:t + 1], scale=-1.0)
            op.then_inc(exp_ready, 1)

        def pt_out(i, u, h):
            g = H * (2 * i + u) + h
            wait_past(act, pv_in_psum, g - 1)
            act.wait_ge(pt_in_psum, g + 1)
            act.activation(pt[:, h % 2], ps_pt[:, h % 2], ACT.Copy).then_inc(pt_ready, 1)

        normalise(0, 0)
        for half in range(2):
            h2t_high(0, 0, half)
        qk_high(0, 0, 0)

        def pieces(i, u, at, last):
            ni, nu = nxt(i, u)
            if at in FIRST_V:
                v_high(i, u, FIRST_V.index(at))
            for t in FIRST_QK:
                if at == FIRST_QK[t]:
                    qk_high(i, u, t)
            if at == AT_NORM[0] and not last:
                normalise(ni, nu)
            for half in range(2):
                if at == OUT[f"o{half}"][0]:
                    ot_high(i, u, half)
            if at == OUT["qk3"][0]:
                qk_high(i, u, 3)
            if last:
                return
            for half in range(2):
                if at == OUT[f"h{half}"][0]:
                    h2t_high(ni, nu, half)
            for t in AT_QK:
                if at == OUT[f"qk{t}"][0]:
                    qk_high(ni, nu, t)
            for t in AT_V:
                if at == OUT[f"v{t}"][0]:
                    v_high(ni, nu, t)

        def slot(i, u, s, last, last_pair):
            pieces(i, u, s + EARLY, last)
            if head := head_at(i, u, s + LEAD, last):
                softmax_exp(*head)
            pieces(i, u, s + MID, last)
            if head := head_at(i, u, s + 2, last):
                pt_out(*head)
            pieces(i, u, s + LATE, last)

        run(act, slot)

    @block.vector
    def _(dve):
        def residual_one(i, u):
            b = 2 * i + u
            dve.wait_ge(landed[u], 32 * (i + 1))
            for t in range(NT):
                dve.wait_ge(y_in_psum, NT * b + t + 1)
                dve.scalar_tensor_tensor(out=x1[:, u, t], in0=ps_g[:, t], scalar=0.0, in1=x_in[:, u, t],
                                         op0=ALU.max, op1=ALU.add).then_inc(x1_ready, 1)

        def row_moments(i, u):
            b = 2 * i + u
            wait_past(dve, moments_ready, b)
            wait_past(dve, ln_ready, b)
            dve.wait_ge(x1_ready, NT * (b + 1))
            for t in range(NT):
                op = dve.bn_stats(partials[:, t], x1[:, u, t])
            op.then_inc(partials_ready, 1)
            wait_alone(dve, partials_ready, b + 1)
            for t in range(NT):
                op = dve.bn_aggr(moments[:, t], partials[:, t])
            op.then_inc(moments_ready, 1)

        def normalise(i, u):
            b = 2 * i + u
            wait_past(dve, h2t_in_psum, 2 * b)
            dve.wait_ge(ln_ready, b + 1)
            dve.tensor_scalar(h2[:, 1], x1[:, u, 1], ln_scale[:, 1:2], ln_shift[:, 1:2], ALU.mult, ALU.add
                              ).then_inc(h2_ready[1], 1)

        def h2t_low(i, u, half):
            dve.wait_ge(h2t_hi_ready, 2 * (2 * i + u) + half + 1)
            dve.scalar_tensor_tensor(out=h2t[:, 1, 2 * half:2 * half + 2].rearrange("p k n -> p (k n)"),
                                     in0=ps_g[:, H_BANK[half]], scalar=0.0,
                                     in1=h2t[:, 0, 2 * half:2 * half + 2].rearrange("p k n -> p (k n)").bitcast(F32),
                                     op0=ALU.max, op1=ALU.subtract).then_inc(h2t_lo_ready, 1)

        def qk_low(i, u, t):
            dve.wait_ge(qk_hi_ready, KT * (2 * i + u) + t + 1)
            dve.scalar_tensor_tensor(out=q[:, u, 1, t], in0=ps_g[:, QK_BANK[t], 0:N], scalar=SCALE,
                                     in1=q[:, u, 0, t].bitcast(F32), op0=ALU.mult, op1=ALU.subtract)
            dve.tensor_tensor(k_[:, u, 1, t], ps_g[:, QK_BANK[t], N:2 * N], k_[:, u, 0, t].bitcast(F32),
                              ALU.subtract).then_inc(qk_lo_ready, 1)

        def v_remainder(i, u, t):
            dve.wait_ge(v1_ready, NT * (2 * i + u) + t + 1)
            dve.tensor_tensor(v_rest[:, t].rearrange("p (h d) -> p h d", h=H), ps_g[:, t].rearrange("p (h d) -> p h d", h=H),
                              v[:, u, t, :, 0:HD], ALU.subtract).then_inc(v_rest_ready, 1)

        def add_bias(i, u, h):
            g = H * (2 * i + u) + h
            wait_past(dve, exp_ready, g - 1)
            wait_past(dve, nonzero_ready, g - 1)
            if h == 0:
                dve.wait_ge(bias_ready, 2 * i + u + 1)
            wait_alone(dve, scores_in_psum, g + 1)
            for t in range(NT):
                op = dve.tensor_tensor_reduce(a[:, h % 2, t], ps_s[:, h % 2, t], bias[:, u, t], -1.0, BIG,
                                              ALU.add, ALU.min, least[:, h % 4, t:t + 1])
            op.then_inc(biased_ready, 1)

        def find_nonzero(i, u, h):
            g = H * (2 * i + u) + h
            dve.wait_ge(biased_ready, g + 1)
            dve.tensor_reduce(nonzero[:, u, :, h], a[:, h % 2], AX_X, ALU.max,
                              apply_absolute_value=True).then_inc(nonzero_ready, 1)

        def gather_two(i, u, c):
            n = H // 2 * (2 * i + u) + c
            dve.wait_ge(pv_in_psum, 2 * (n + 1))
            wait_past(dve, o_ready, n)
            heads = ps_o[:, c % 2, 0:2 * NT * VW].rearrange("p (t h w) -> p (t h) w", t=NT, h=2)
            dve.tensor_reduce(o_raw[:].rearrange("p t h d -> p (t h) d"),
                              heads[:, :, 0:3 * HD].rearrange("p h (c d) -> p h d c", c=3), AX_X, ALU.add)
            dve.reciprocal(row_sum[:].rearrange("p t h -> p (t h)"), heads[:, :, 3 * HD]).then_inc(o_raw_ready, 1)
            dve.wait_ge(o_raw_ready, n + 1)
            dve.scalar_tensor_tensor(out=row_scale[:], in0=nonzero[:, u, :, 2 * c:2 * c + 2], scalar=0.0, in1=row_sum[:],
                                     op0=ALU.is_gt, op1=ALU.mult).then_inc(row_scale_ready, 1)
            dve.wait_ge(row_scale_ready, n + 1)
            if c == 0:
                wait_past(dve, ot_in_psum, 2 * (2 * i + u))
            dve.tensor_tensor(o[:, :, 2 * c:2 * c + 2], o_raw[:], row_scale[:].unsqueeze(3).to_broadcast([P, NT, 2, HD]),
                              ALU.mult).then_inc(o_ready, 1)

        def ot_low(i, u, half):
            dve.wait_ge(ot_hi_ready, 2 * (2 * i + u) + half + 1)
            dve.tensor_tensor(ot[:, 1, 2 * half:2 * half + 2].rearrange("p k n -> p (k n)"), ps_g[:, half],
                              ot[:, 0, 2 * half:2 * half + 2].rearrange("p k n -> p (k n)").bitcast(F32),
                              ALU.subtract).then_inc(ot_lo_ready, 1)

        def residual_two(i, u, t):
            wait_past(dve, stored[u], 16 * NT * i)
            dve.wait_ge(projected, NT * (2 * i + u) + t + 1)
            dve.tensor_tensor(result[:, u, t], ps_g[:, t], x1[:, u, t], ALU.add).then_inc(result_ready, 1)

        residual_one(0, 0)
        row_moments(0, 0)
        normalise(0, 0)
        for half in range(2):
            h2t_low(0, 0, half)
        qk_low(0, 0, 0)

        def pieces(i, u, at, last):
            ni, nu = nxt(i, u)
            if at in FIRST_V:
                v_remainder(i, u, FIRST_V.index(at))
            for t in FIRST_QK:
                if at == FIRST_QK[t]:
                    qk_low(i, u, t)
            if at == AT_NORM[1] and not last:
                normalise(ni, nu)
            for half in range(2):
                if at == OUT[f"o{half}"][1]:
                    ot_low(i, u, half)
            if at == OUT["qk3"][1]:
                qk_low(i, u, 3)
            for t in AT_PROJECT:
                if at == AT_PROJECT[t][1]:
                    residual_two(i, u, t)
            if last:
                return
            for half in range(2):
                if at == OUT[f"h{half}"][1]:
                    h2t_low(ni, nu, half)
            for t in AT_QK:
                if at == OUT[f"qk{t}"][1]:
                    qk_low(ni, nu, t)
            for t in AT_V:
                if at == OUT[f"v{t}"][1]:
                    v_remainder(ni, nu, t)

        def slot(i, u, s, last, last_pair):
            pieces(i, u, s + EARLY, last)
            if s == AT_Y - MID and not last:
                residual_one(*nxt(i, u))
            if head := head_at(i, u, s + LEAD, last):
                add_bias(*head)
                if s not in CROWDED:
                    find_nonzero(*head)
            if s == AT_Y - MID and not last:
                row_moments(*nxt(i, u))
            pieces(i, u, s + MID, last)
            pieces(i, u, s + LATE, last)
            if (head := head_at(i, u, s + LEAD, last)) and s in CROWDED:
                find_nonzero(*head)
            for behind in range(2):
                if (head := head_at(i, u, s - behind, last)) and head[2] % 2 == 1 and behind == (head[2] in GATHER_LATER):
                    gather_two(head[0], head[1], head[2] // 2)

        run(dve, slot)

    @block.tensor
    def _(pe):
        def y_back(i, u):
            b = 2 * i + u
            pe.wait_ge(y_ready, b + 1)
            for t in range(NT):
                wait_past(pe, result_ready, NT * (b - 2) + t + 1)
                for k in range(KT):
                    op = pe.transpose(ps_g[:, t, k * P:(k + 1) * P], y[:, u, k, t * P:(t + 1) * P], ident[:])
                op.then_inc(y_in_psum, 1)

        def transpose_h2(i, u, half):
            b = 2 * i + u
            if half == 0:
                for t in range(NT):
                    pe.wait_ge(h2_ready[t], b + 1)
            else:
                wait_past(pe, qk_lo_ready, KT * b)
            for k in range(2 * half, 2 * half + 2):
                for t in range(NT):
                    c = k % 2 * N + t * P
                    op = pe.transpose(ps_g[:, H_BANK[half], c:c + P], h2[:, t, k * P:(k + 1) * P], ident[:])
            op.then_inc(h2t_in_psum, 1)

        def project_qk(i, u, t, w):
            b = 2 * i + u
            if w == 0 and t == 1:
                pe.wait_ge(v_rest_ready, NT * (b + 1))
            if w == 0 and t == 2:
                wait_past(pe, ot_lo_ready, 2 * b - 1)
            for half in range(2):
                if t == 0 and w == 0:
                    pe.wait_ge(h2t_lo_ready, 2 * b + half + 1)
                for s, m in HILO:
                    for k in range(2 * half, 2 * half + 2):
                        op = pe.matmul(ps_g[:, QK_BANK[t], w * N:(w + 1) * N],
                                       (attn_hi, attn_lo)[s][:, w * KT + k, t * P:(t + 1) * P], h2t[:, m, k],
                                       start=((s, m) == HILO[0] and k == 0), stop=((s, m) == HILO[2] and k == KT - 1))
            if w == 1:
                op.then_inc(qk_in_psum, 1)

        def last_qk(i, u, w, last):
            if w == 0 and last:
                pe.wait_ge(result_ready, NT * (2 * i + u))
            elif w == 0:
                pe.wait_ge(x1_ready, NT * (2 * i + u + 1) + 1)
            project_qk(i, u, KT - 1, w)

        def project_v(i, u, t, half):
            if half == 0 and t == 1:
                pe.wait_ge(qk_lo_ready, KT * (2 * i + u) + 1)
            for s, m in HILO:
                for k in range(2 * half, 2 * half + 2):
                    op = pe.matmul(ps_g[:, t], h2t[:, s, k, t * P:(t + 1) * P], (attn_hi, attn_lo)[m][:, 2 * KT + k],
                                   start=((s, m) == HILO[0] and k == 0), stop=((s, m) == HILO[2] and k == KT - 1))
            if half == 1:
                op.then_inc(v_in_psum, 1)

        def score(i, u, h):
            g = H * (2 * i + u) + h
            wait_past(pe, biased_ready, g - 1)
            pe.wait_ge(qk_lo_ready, KT * (2 * i + u) + h // HPT + 1)
            rows = slice(h % HPT * HD, h % HPT * HD + HD)
            for t in range(NT):
                for n, (s, m) in enumerate(HILO):
                    op = pe.matmul(ps_s[:, h % 2, t], q[rows, u, s, h // HPT, t * P:(t + 1) * P], k_[rows, u, m, h // HPT],
                                   start=(n == 0), stop=(n == 2))
            op.then_inc(scores_in_psum, 1)

        def transpose_prob(i, u, h):
            g = H * (2 * i + u) + h
            wait_past(pe, pt_ready, g - 1)
            pe.wait_ge(p_lo_ready, g + 1)
            for part in range(2):
                for m in range(NT):
                    for t in range(NT):
                        op = pe.transpose(ps_pt[:, h % 2, part, m, t * P:(t + 1) * P],
                                          prob16[:, h % 4, part, t, m * P:(m + 1) * P], ident16[:])
            op.then_inc(pt_in_psum, 1)

        def times_v(i, u, h):
            b = 2 * i + u
            g = H * b + h
            if h == 0:
                pe.wait_ge(v3_ready, NT * (b + 1))
            if h % 2 == 0:
                wait_past(pe, o_raw_ready, H // 2 * b + h // 2 - 1)
            pe.wait_ge(pt_ready, g + 1)
            for t in range(NT):
                c = (2 * t + h % 2) * VW
                for n, (part, m) in enumerate([(part, m) for part in range(2) for m in range(NT)]):
                    op = pe.matmul(ps_o[:, h // 2 % 2, c:c + VW], pt[:, h % 2, part, m, t * P:(t + 1) * P], v[:, u, m, h],
                                   start=(n == 0), stop=(n == 3))
            op.then_inc(pv_in_psum, 1)

        def transpose_o(i, u, half, last):
            b = 2 * i + u
            pe.wait_ge(o_ready, H // 2 * b + 4 * half + 4)
            if last and half == 0:
                pe.wait_ge(qk_lo_ready, KT * (b + 1))
            elif half == 0:
                pe.wait_ge(v_rest_ready, NT * (b + 1) + 1)
            elif not last:
                pe.wait_ge(qk_lo_ready, KT * (b + 1) + 2)
            flat = o[:].rearrange("p t h d -> p t (h d)")
            for k in range(2 * half, 2 * half + 2):
                for t in range(NT):
                    c = k % 2 * N + t * P
                    op = pe.transpose(ps_g[:, half, c:c + P], flat[:, t, k * P:(k + 1) * P], ident[:])
            op.then_inc(ot_in_psum, 1)

        def project_o(i, u, t, half, last):
            b = 2 * i + u
            if t == 0:
                pe.wait_ge(ot_lo_ready, 2 * b + half + 1)
            if t == 0 and half == 0 and not last:
                pe.wait_ge(qk_lo_ready, KT * (b + 1) + 3)
            for s, m in HILO:
                for k in range(2 * half, 2 * half + 2):
                    op = pe.matmul(ps_g[:, t], ot[:, s, k, t * P:(t + 1) * P], (attn_hi, attn_lo)[m][:, 3 * KT + k],
                                   start=((s, m) == HILO[0] and k == 0), stop=((s, m) == HILO[2] and k == KT - 1))
            if half == 1:
                op.then_inc(projected, 1)

        y_back(0, 0)
        for half in range(2):
            transpose_h2(0, 0, half)
        for w in range(2):
            project_qk(0, 0, 0, w)

        def pieces(i, u, at, last):
            ni, nu = nxt(i, u)
            if at == FIRST_V[1]:
                pe.wait_ge(ones_ready, 1)
            if at in FIRST_V:
                for half in range(2):
                    project_v(i, u, FIRST_V.index(at), half)
            for t in FIRST_QK:
                if at == FIRST_QK[t]:
                    for w in range(2):
                        project_qk(i, u, t, w)
            if at in AT_O:
                transpose_o(i, u, AT_O.index(at), last)
            if at in AT_QK3:
                last_qk(i, u, AT_QK3.index(at), last)
            for t in AT_PROJECT:
                for half in range(2):
                    if at == AT_PROJECT[t][half]:
                        project_o(i, u, t, half, last)
            if last:
                return
            if at == AT_Y:
                y_back(ni, nu)
            if at in AT_H:
                transpose_h2(ni, nu, AT_H.index(at))
            for t in AT_QK:
                if at in AT_QK[t]:
                    project_qk(ni, nu, t, AT_QK[t].index(at))
            for t in AT_V:
                for half in range(2):
                    if at == AT_V[t][half]:
                        project_v(ni, nu, t, half)

        def slot(i, u, s, last, last_pair):
            pieces(i, u, s + EARLY, last)
            if head := head_at(i, u, s + LEAD, last):
                score(*head)
            pieces(i, u, s + MID, last)
            if head := head_at(i, u, s, last):
                times_v(*head)
            if head := head_at(i, u, s + 2, last):
                transpose_prob(*head)
            pieces(i, u, s + LATE, last)

        run(pe, slot)


def kernel(**inputs):
    import numpy as np
    import concourse.bacc as bacc
    from concourse.bass_utils import run_bass_kernel_spmd

    def tiled(a):
        return a.reshape(E, KT, P).transpose(2, 0, 1)

    arrays = {
        "x": inputs["x"],
        "adj": inputs["adj"],
        "adj_t": inputs["adj"].transpose(0, 2, 1),
        "router_w": inputs["L0_gnn_router_w"],
        "router_b": inputs["L0_gnn_router_b"].reshape(1, E),
        "expert_w": inputs["L0_gnn_expert_w"],
        "gamma": tiled(inputs["L0_gnn_bn_gamma"]),
        "beta": tiled(inputs["L0_gnn_bn_beta"]),
        "attn_w": np.stack([inputs[f"L1_gnn_W{c}"].T for c in "qkvo"]),
    }
    arrays = {f"in_{name}": np.ascontiguousarray(a) for name, a in arrays.items()}
    nc = bacc.Bacc("TRN2", target_bir_lowering=False, num_devices=1)
    args = [nc.dram_tensor(name, a.shape, mybir.dt.from_np(a.dtype), kind="ExternalInput").ap() for name, a in arrays.items()]
    out = nc.dram_tensor("out", (B, N, D), F32, kind="ExternalOutput").ap()
    build(nc, *args, out)
    return run_bass_kernel_spmd(nc, [arrays], core_ids=[0]).results[0]["out"]
```
